# Optimizing a Trainium2 kernel written in Bass

```python
import numpy as np
import jax
import jax.numpy as jnp

def _softmax(x, axis=-1):
    return jax.nn.softmax(x, axis=axis)

def _gelu(x):
    return jax.nn.gelu(x, approximate=True)

def _silu(x):
    return jax.nn.silu(x)

def _sigmoid(x):
    return jax.nn.sigmoid(x)

def _layernorm(x, axis=-1, eps=1e-05):
    m = jnp.mean(x, axis=axis, keepdims=True)
    v = jnp.var(x, axis=axis, keepdims=True)
    return (x - m) / jnp.sqrt(v + eps)

def _scatter_add(tgt, idx, src, axis=0):
    return tgt.at[idx].add(src)

def _segment_sum(src, seg, n):
    return jax.ops.segment_sum(src, seg, n)
kernel_name = 'mk_decoder_postln_d1_seqx_r4_3b62a7'

def setup_inputs(seed: int=0):
    np.random.seed(seed)
    _w = jnp.asarray

    def _rec_inputs():
        import jax
        import jax.numpy as jnp
        _rk = jax.random.key(seed)
        x = 7.22e-05 + 1 * jax.random.normal(jax.random.fold_in(_rk, 1), (16, 256, 512), jnp.float32)
        _lenS = 256 - jax.random.randint(jax.random.fold_in(_rk, 7), (16,), 0, max(1, 256 // 4) + 1, jnp.int32)
        _lenS2 = 256 - jax.random.randint(jax.random.fold_in(_rk, 8), (16,), 0, max(1, 256 // 4) + 1, jnp.int32)
        _ctx_2048P = jax.random.normal(jax.random.fold_in(_rk, 11), (16, 16, 512), jnp.float32)
        _ctx_2048c = jax.random.dirichlet(jax.random.fold_in(_rk, 511), 0.3 * jnp.ones((16,), jnp.float32), (16, 256))
        _ctx_2048t = jnp.einsum('bsk,bkd->bsd', _ctx_2048c, _ctx_2048P)
        _ctx_2048t = _ctx_2048t * jax.lax.rsqrt(jnp.mean(jnp.square(_ctx_2048t)) + 1e-12) * 0.953939
        ctx_2048 = 4.13588e-05 + 0.999923 * (_ctx_2048t + 0.3 * jax.random.normal(jax.random.fold_in(_rk, 611), (16, 256, 512), jnp.float32))
        return (x, ctx_2048)
    x, ctx_2048 = _rec_inputs()

    def _L0_attn_setup():
        import jax, jax.numpy as jnp
        import numpy as np
        E = 512
        H = 3
        key = jax.random.key(seed)
        ks = jax.random.split(key, 6)
        B, N = (4, 512)
        x = jax.random.normal(ks[0], (B, N, E), dtype=jnp.float32)
        Wq = jax.random.normal(ks[1], (H, E, E), dtype=jnp.float32) * 0.02
        Wk = jax.random.normal(ks[2], (H, E, E), dtype=jnp.float32) * 0.02
        Wv = jax.random.normal(ks[3], (H, E, E), dtype=jnp.float32) * 0.02
        fc_w = jax.random.normal(ks[4], (E, E), dtype=jnp.float32) * 0.02
        fc_b = jax.random.normal(ks[5], (E,), dtype=jnp.float32) * 0.02
        return {'x': x, 'Wq': Wq, 'Wk': Wk, 'Wv': Wv, 'fc_w': fc_w, 'fc_b': fc_b}
    _L0_attn_all = _L0_attn_setup()
    _L0_attn_in = {k: v for k, v in _L0_attn_all.items() if k in ('Wq', 'Wk', 'Wv', 'fc_w', 'fc_b')}
    del _L0_attn_all

    def _L0_xattn_setup():
        import jax, jax.numpy as jnp
        import numpy as np
        N_HEAD = 8
        key = jax.random.key(seed)
        k1, k2, k3 = jax.random.split(key, 3)
        B, D, L = (4, 256, 512)
        q = jax.random.normal(k1, (B, D, L), dtype=jnp.float32)
        k = jax.random.normal(k2, (B, D, L), dtype=jnp.float32)
        v = jax.random.normal(k3, (B, D, L), dtype=jnp.float32)
        gamma = jnp.ones((), dtype=jnp.float32)
        return {'q': q, 'k': k, 'v': v, 'gamma': gamma}
    _L0_xattn_all = _L0_xattn_setup()
    _L0_xattn_in = {k: v for k, v in _L0_xattn_all.items() if k in ('gamma',)}
    del _L0_xattn_all

    def _L0_ffn_setup():
        import jax, jax.numpy as jnp
        import numpy as np
        D_MODEL = 512
        D_EXPERT = 2048
        EPS = 1e-08

        def ternary_quant(w):
            scale = jnp.mean(jnp.abs(w)) + EPS
            q = jnp.clip(jnp.round(w / scale), -1.0, 1.0) * scale
            return w + jax.lax.stop_gradient(q - w)
        key = jax.random.key(seed)
        k_x, k_up, k_gate, k_down = jax.random.split(key, 4)
        std_in = 1.0 / np.sqrt(D_MODEL)
        std_exp = 1.0 / np.sqrt(D_EXPERT)
        return {'x': jax.random.normal(k_x, (4, 512, D_MODEL), dtype=jnp.float32), 'W_up': jax.random.normal(k_up, (D_EXPERT, D_MODEL), dtype=jnp.float32) * std_in, 'W_gate': jax.random.normal(k_gate, (D_EXPERT, D_MODEL), dtype=jnp.float32) * std_in, 'W_down': jax.random.normal(k_down, (D_MODEL, D_EXPERT), dtype=jnp.float32) * std_exp}
    _L0_ffn_all = _L0_ffn_setup()
    _L0_ffn_in = {k: v for k, v in _L0_ffn_all.items() if k in ('W_up', 'W_gate', 'W_down')}
    del _L0_ffn_all
    return {'x': x, 'ctx_2048': ctx_2048, 'L0_attn_Wq': _L0_attn_in['Wq'], 'L0_attn_Wk': _L0_attn_in['Wk'], 'L0_attn_Wv': _L0_attn_in['Wv'], 'L0_attn_fc_w': _L0_attn_in['fc_w'], 'L0_attn_fc_b': _L0_attn_in['fc_b'], 'L0_xattn_gamma': _L0_xattn_in['gamma'], 'L0_ffn_W_up': _L0_ffn_in['W_up'], 'L0_ffn_W_gate': _L0_ffn_in['W_gate'], 'L0_ffn_W_down': _L0_ffn_in['W_down']}

def reference(x, ctx_2048, L0_attn_Wq, L0_attn_Wk, L0_attn_Wv, L0_attn_fc_w, L0_attn_fc_b, L0_xattn_gamma, L0_ffn_W_up, L0_ffn_W_gate, L0_ffn_W_down):
    import jax
    import jax.numpy as jnp

    def _L0_attn_ref(x, Wq, Wk, Wv, fc_w, fc_b):
        import jax, jax.numpy as jnp
        import numpy as np
        E = 512
        H = 3
        Q = jnp.einsum('bne,hde->hbnd', x, Wq)
        K = jnp.einsum('bne,hde->hbnd', x, Wk)
        V = jnp.einsum('bne,hde->hbnd', x, Wv)
        scale = 1.0 / jnp.sqrt(jnp.float32(E))
        scores = jnp.einsum('hbnd,hbmd->hbnm', Q, K) * scale
        w = jax.nn.softmax(scores, axis=2)
        attn = jnp.einsum('hbnm,hbmd->hbnd', w, V)
        mean = jnp.mean(attn, axis=0)
        return mean @ fc_w.T + fc_b

    def _L0_xattn_ref(q, k, v, gamma):
        import jax, jax.numpy as jnp
        import numpy as np
        N_HEAD = 8
        B, Dq, Lq = q.shape
        Dv, Lk = (v.shape[-2], v.shape[-1])
        h = N_HEAD
        dq = Dq // h
        dv = Dv // h
        qh = q.reshape(B, h, dq, Lq)
        kh = k.reshape(B, h, dq, Lk)
        vh = v.reshape(B, h, dv, Lk)
        scale = 1.0 / jnp.sqrt(jnp.asarray(dq, dtype=q.dtype))
        qk = jnp.einsum('bhdq,bhdl->bhql', qh, kh) * scale
        sm = jax.nn.softmax(qk, axis=-1)
        ret = jnp.einsum('bhql,bhdl->bhdq', sm, vh)
        ret = ret.reshape(B, Dv, Lq)
        return gamma * ret

    def _L0_ffn_ref(x, W_up, W_gate, W_down):
        import jax, jax.numpy as jnp
        import numpy as np
        D_MODEL = 512
        D_EXPERT = 2048
        EPS = 1e-08

        def ternary_quant(w):
            scale = jnp.mean(jnp.abs(w)) + EPS
            q = jnp.clip(jnp.round(w / scale), -1.0, 1.0) * scale
            return w + jax.lax.stop_gradient(q - w)
        wu = ternary_quant(W_up)
        wg = ternary_quant(W_gate)
        wd = ternary_quant(W_down)
        up = jnp.einsum('bsd,ed->bse', x, wu)
        gate = jnp.einsum('bsd,ed->bse', x, wg)
        hidden = jax.nn.silu(up) * gate
        return jnp.einsum('bse,de->bsd', hidden, wd)
    x = _layernorm(x + _L0_attn_ref(x, L0_attn_Wq, L0_attn_Wk, L0_attn_Wv, L0_attn_fc_w, L0_attn_fc_b), axis=-1)
    x = _layernorm(x + _L0_xattn_ref(x, ctx_2048, ctx_2048, L0_xattn_gamma), axis=-1)
    x = _layernorm(x + _L0_ffn_ref(x, L0_ffn_W_up, L0_ffn_W_gate, L0_ffn_W_down), axis=-1)
    return x

_drawn_inputs = setup_inputs


def setup_inputs(seed=0):
    import zlib

    import numpy as np

    out = dict(_drawn_inputs(seed))
    spreads = {}
    factors = {'L0_attn_Wq': 8.0, 'L0_attn_Wk': 8.0, 'L0_attn_Wv': 3.559, 'L0_attn_fc_w': 3.522}
    for name, (base, spread) in spreads.items():
        noise = np.random.default_rng([zlib.crc32(name.encode()), seed]).standard_normal(out[name].shape)
        drawn = base * np.exp(spread * noise) if base else spread * noise
        out[name] = jnp.asarray(drawn.astype(out[name].dtype))
    for name, factor in factors.items():
        out[name] = (out[name] * factor).astype(out[name].dtype)
    return out
```

```python
from contextlib import ExitStack

import concourse.bass as bass
from concourse import mybir

F32 = mybir.dt.float32
F16 = mybir.dt.float16
ACT = mybir.ActivationFunctionType
ALU = mybir.AluOpType
AXX = mybir.AxisListType.X
RMAX = bass.bass_isa.ReduceOp.max

P = 128
EPS_LN = 1e-5
EPS_Q = 1e-8


class Signal:

    def __init__(self, sem, per, by=1):
        self.sem, self.per, self.by = sem, per, by

    def at(self, batch, count):
        return (batch * self.per + count) * self.by


def decoder_layer(nc, x, xT, ctx_n, ctx_t, wq, wk, wv, fcT, fcb, gamma, wu, wg, wd, out):
    B, N, E = x.shape
    H = wq.shape[0]
    F = wu.shape[1]
    KT = E // P
    MT = N // P
    DH = 32
    XH = N // DH
    HG = P // DH
    FT = F // P
    PAIRS = FT // 2
    assert (E, N, XH, PAIRS, H, MT, KT) == (512, 256, 8, 8, 3, 2, 4)

    TOP = 1024.0
    DOWN = 2.0 ** -14
    WTOP = 4096.0
    QS = 64.0
    KTOP = 4096.0
    MROW = 4096.0
    X2S = 32.0
    HS = 2.0 ** -13
    ESC = 1.0 / (DOWN * TOP ** 3 * E ** 0.5)
    ASC = 1.0 / (DOWN * WTOP * H * TOP ** 2)
    XSC = 1.0 / (QS * KTOP * DH ** 0.5)
    DSC = 1.0 / (HS * X2S * X2S)

    BLOCKS = [("G", 0, 0), ("G", 0, 1), ("G", 1, 0), ("G", 1, 1), ("S", 0, 0), ("G", 2, 0), ("G", 2, 1),
              ("S", 1, 0), ("S", 2, 0)] + [("V", h, m) for h in range(H) for m in range(MT)]
    GV = [j for j, b in enumerate(BLOCKS) if b[0] != "S"]
    SB = [j for j, b in enumerate(BLOCKS) if b[0] == "S"]
    NBLK = len(BLOCKS)
    NGV = len(GV)
    TILES = XH * KT
    S1_FROM = 4
    s1_of = {j: range(3 * (j - S1_FROM), min(3 * (j - S1_FROM) + 3, TILES)) for j in range(S1_FROM, NBLK)}
    assert s1_of[NBLK - 1].stop == TILES

    with ExitStack() as ctx:
        def sb(name, shape, dt):
            return ctx.enter_context(nc.sbuf_tensor(name, shape, dt))

        def signal(name, per, by=1):
            return Signal(ctx.enter_context(nc.semaphore(name)), per, by)

        bank = {n: ctx.enter_context(nc.psum_tensor("bank_" + n, [P, 512], F32))
                for n in ("L0", "L1", "S0", "S1", "U", "G", "O", "T")}
        L = [bank["L0"], bank["L1"]]
        S = [bank["S0"], bank["S1"]]
        T16 = bank["T"][:, :].bitcast(F16)

        A = sb("score_matrix", [P, 2, H, KT, E], F16)
        Bm = sb("value_matrix", [P, 2, H, KT, E], F16)
        Wu = sb("ternary_up", [P, KT, F], F16)
        Wg = sb("ternary_gate", [P, KT, F], F16)
        Wd = sb("ternary_down", [P, FT, E], F16)
        stage = sb("stage", [P, 1024], F32)
        xTs = sb("xT_split", [P, 2, KT, N], F16)
        xn = sb("x_rows", [P, MT, E], F32)
        work_a = sb("work_a", [P, 6144], F32)
        work_b = sb("work_b", [P, 6144], F32)
        work_c = sb("work_c", [P, 8192], F32)
        keys_t = sb("ctx_columns", [P, KT, N], F32)
        ksplit = sb("key_split", [P, 2, MT, E], F16)
        Gs = work_a[:, 0:2048].bitcast(F16).rearrange("p (b s k n) -> p b s k n", b=2, s=2, k=KT)
        Vs = work_a[:, 2048:5120].bitcast(F16).rearrange("p (s h m e) -> p s h m e", s=2, h=H, m=MT)
        we = work_a[:, 5120:6144].rearrange("p (b m n) -> p b m n", b=2, m=MT)
        den = work_a[:, 5120:5632]
        x1 = work_b[:, 0:1024].rearrange("p (m e) -> p m e", m=MT)
        hl = work_b[:, 1024:2048].bitcast(F16).rearrange("p (s m e) -> p s m e", s=2, m=MT)
        Qst = work_b[:, 2048:4096].bitcast(F16).rearrange("p (h e) -> p h e", h=XH)
        Kst = work_b[:, 4096:6144].bitcast(F16).rearrange("p (h e) -> p h e", h=XH)
        Pe = work_c[:, 0:2048].rearrange("p (v e) -> p v e", v=HG)
        Psum = work_c[:, 2048:4096].rearrange("p (v e) -> p v e", v=HG)
        x2 = work_c[:, 4096:5120].rearrange("p (m e) -> p m e", m=MT)
        x2T = work_c[:, 5120:6144].bitcast(F16).rearrange("p (s k n) -> p s k n", s=2, k=KT)
        hs = work_c[:, 6144:7168].bitcast(F16).rearrange("p (b s e n) -> p b s e n", b=2, s=2, e=2)
        th = work_c[:, 7168:8192].rearrange("p (b e) -> p b e", b=2)
        ws = sb("weight_split", [P, 2, H, MT, N], F16)
        fcb_b = sb("fcb_b", [P, E], F32)
        gam = sb("gam", [P, 1], F32)
        ones = sb("ones", [P, P], F32)
        id16 = sb("id16", [P, P], F16)
        id32 = sb("id32", [P, P], F32)
        mhalf = sb("mhalf", [P, MT], F32)
        eps = sb("eps", [P, MT], F32)
        nm = sb("neg_max_rows", [TILES, 2, P], F16)
        xmx = sb("cross_max", [P, TILES], F32)
        cm = sb("col_max", [P, H, MT], F32)
        nb = sb("exp_bias", [P, H, MT], F32)
        sm = sb("exp_sum", [P, H, MT], F32)
        rs = sb("exp_sum_inv", [P, H, MT], F32)
        r4 = sb("weight_scale", [P, H, MT], F32)
        bst = [sb(f"bn{r}", [P, MT, 6], F32) for r in range(3)]
        mv = [sb(f"mean_var{r}", [P, MT, 2], F32) for r in range(3)]
        ve = [sb(f"var_eps{r}", [P, MT], F32) for r in range(3)]
        rstd = [sb(f"rstd{r}", [P, MT], F32) for r in range(3)]
        sc = sb("scales", [P, 24], F32)
        (am_x, amr_x, inv_x, s_x, sq_x, esc, asc, am_c, amr_c, inv_c, s_c, xsc, c_esc, c_asc, am_w, amr_w,
         inv_w, s_w) = (sc[:, n:n + 1] for n in range(18))
        part = sb("abs_parts", [P, 3, 16], F32)
        tot = sb("abs_total", [P, 3], F32)
        mean_w = sb("weight_mean", [P, 3], F32)
        thr = sb("threshold", [P, 3], F32)
        nthr = sb("neg_threshold", [P, 3], F32)
        fsc = sb("ffn_scales", [P, 4], F32)
        half_u, gd, dsc = (fsc[:, n:n + 1] for n in range(3))

        ring = [work_a[:, 0:2048], work_a[:, 2048:4096], work_a[:, 4096:6144]]
        hold = work_b[:, :].rearrange("p (h k e) -> p h k e", h=H, k=KT)
        stg = work_c[:, :].rearrange("p (c f) -> p c f", c=4)

        consts = signal("consts", 0)
        small_ld = signal("small_ld", 0, 16)
        w_ld = [signal(f"w_ld{n}", 0, 16) for n in range(3)]
        ab_mm = signal("ab_mm", 0)
        ab_ev = signal("ab_ev", 0)
        f_ld = [signal(f"f_ld{n}", 0, 16) for n in range(4)]
        f_abs = signal("f_abs", 0)
        f_tot = signal("f_tot", 0)
        f_mm = signal("f_mm", 0)
        prep = signal("prep", 0)
        am_w_rdy = signal("am_w_rdy", 0)
        amr_w_rdy = signal("amr_w_rdy", 0)
        sw_rdy = signal("sw_rdy", 0)
        ab_hi = signal("ab_hi", 0)
        ab_lo = signal("ab_lo", 0)
        quant = signal("quant", 0)
        krow = signal("krow", 0)
        xT_ld = signal("xT_ld", 1, 16)
        am_x_rdy = signal("am_x_rdy", 1)
        amr_x_rdy = signal("amr_x_rdy", 1)
        xs_step = signal("xs_step", 5)
        xT_hi = signal("xT_hi", 1)
        xT_lo = signal("xT_lo", 1)
        xn_ld = signal("xn_ld", 1, 16)
        xb_rdy = signal("xb_rdy", 1)
        l_mm = signal("l_mm", NBLK + MT)
        gv_hi = signal("gv_hi", NGV)
        gv_lo = signal("gv_lo", NGV)
        cmax = signal("cmax", H)
        bias_rdy = signal("bias_rdy", H)
        e_done = signal("e_done", H)
        sum_inv = signal("sum_inv", H)
        wsc_rdy = signal("wsc_rdy", H)
        w_hi = signal("w_hi", H)
        w_lo = signal("w_lo", H)
        y1_rdy = signal("y1_rdy", MT)
        x1_rdy = signal("x1_rdy", 1)
        q_hi = signal("q_hi", 1)
        q_lo = signal("q_lo", 1)
        q_st = signal("q_st", 3 * HG, 16)
        c_ld = signal("c_ld", 1, 16)
        am_c_rdy = signal("am_c_rdy", 1)
        amr_c_rdy = signal("amr_c_rdy", 1)
        cs_step = signal("cs_step", 3)
        k_hi = signal("k_hi", 1)
        k_lo = signal("k_lo", 1)
        k_st = signal("k_st", 3 * HG, 16)
        ct_ld = signal("ct_ld", 1, 16)
        xsc_rdy = signal("xsc_rdy", 1)
        s1_mm = signal("s1_mm", TILES)
        s1_max = signal("s1_max", TILES)
        nt_mm = signal("nt_mm", 1)
        nm_hi = signal("nm_hi", 1)
        nm_lo = signal("nm_lo", 1)
        nm_st = signal("nm_st", 2, 16)
        s2_mm = signal("s2_mm", TILES)
        s2_exp = signal("s2_exp", TILES)
        p_add = signal("p_add", TILES)
        pv_mm = signal("pv_mm", 8)
        den_mm = signal("den_mm", MT)
        den_inv = signal("den_inv", MT)
        o_read = signal("o_read", MT)
        x1_copy = signal("x1_copy", 1)
        y2_rdy = signal("y2_rdy", MT)
        x2_rdy = signal("x2_rdy", 1)
        x2_hi = signal("x2_hi", 1)
        x2_lo = signal("x2_lo", 1)
        xt_mm = signal("xt_mm", 2)
        xt_ev = signal("xt_ev", 2)
        u_mm = signal("u_mm", PAIRS)
        g_mm = signal("g_mm", PAIRS)
        th_rdy = signal("th_rdy", PAIRS)
        t_rdy = signal("t_rdy", PAIRS)
        p_rdy = signal("p_rdy", PAIRS)
        h_hi = signal("h_hi", PAIRS)
        h_lo = signal("h_lo", PAIRS)
        dn_mm = signal("dn_mm", PAIRS)
        y3_rdy = signal("y3_rdy", MT)
        out_rdy = signal("out_rdy", 1)
        out_st = signal("out_st", 1, 16)
        ln_st = [signal(f"ln_st{r}", MT) for r in range(3)]
        ln_ag = [signal(f"ln_ag{r}", MT) for r in range(3)]
        ln_ve = [signal(f"ln_ve{r}", 1) for r in range(3)]
        ln_rs = [signal(f"ln_rs{r}", 1) for r in range(3)]

        block = ctx.enter_context(nc.Block())

        pause, pause_x, pause_c = (sc[:, n:n + 1] for n in (18, 19, 20))

        def run_stages(eng, stage_of):
            stage_of(0, True, False, False, True)
            stage_of(1, True, True, False, True)
            stage_of(2, True, True, True, True)
            with eng.Fori(3, B - 1) as i:
                stage_of(i, True, True, True, True)
            stage_of(B - 1, True, True, True, False)
            stage_of(B, False, True, True, False)
            stage_of(B + 1, False, False, True, False)

        SEQ = [(wq, 0), (wk, 0), (wq, 1), (wk, 1), (wq, 2), (wk, 2), (fcT, None), (wv, 0), (wv, 1), (wv, 2)]
        SLOT = [0, 1, 2, 0, 1, 2, 0, 1, 2, 1]
        SLOT_READ = {3: KT, 4: KT, 5: 2 * KT, 6: 2 * KT, 7: 3 * KT, 8: 3 * KT, 9: 4 * KT}
        ring_of = lambda n: ring[SLOT[n]]

        @block.sync
        def _(sp):
            sp.dma_start(fcb_b[:, :], fcb.partition_broadcast(P)).then_inc(small_ld.sem, 16)
            sp.dma_start(gam[:, :], gamma.partition_broadcast(P)).then_inc(small_ld.sem, 16)

            def load_w(n):
                w, h = SEQ[n]
                src = (w[h] if h is not None else w).rearrange("(k p) e -> p k e", p=P)
                if n >= 3:
                    sp.wait_ge(ab_mm.sem, ab_mm.at(0, SLOT_READ[n]))
                sp.dma_start(ring_of(n)[:, :].rearrange("p (k e) -> p k e", k=KT), src).then_inc(
                    w_ld[SLOT[n]].sem, 16)

            def load_f(m, c):
                src = [wu, wg, wd][m].rearrange("(k p) f -> p k f", p=P)
                sp.wait_ge(quant.sem, quant.at(0, 4 * (m - 1) + c + 1)) if m else None
                if m < 2:
                    sp.dma_start(stg[:, c, :], src[:, c, :]).then_inc(f_ld[c].sem, 16)
                else:
                    sp.dma_start(stg[:, c, :].rearrange("p (k e) -> p k e", e=E),
                                 src[:, 4 * c:4 * c + 4, :]).then_inc(f_ld[c].sem, 16)

            for n in range(3):
                load_w(n)
            for c in range(4):
                load_f(0, c)
            for n in range(3, 7):
                load_w(n)
            sp.dma_start(stage[:, :].rearrange("p (k n) -> p k n", k=KT),
                         xT[0].rearrange("(k p) n -> p k n", p=P)).then_inc(xT_ld.sem, 16)
            for c in range(4):
                load_f(1, c)
            for n in range(7, 10):
                load_w(n)
            for c in range(4):
                load_f(2, c)

            def stages(i, att, cross, ffn, nxt):
                b = i - 1
                if cross:
                    sp.wait_ge(consts.sem, 7)
                    sp.wait_ge(pv_mm.sem, pv_mm.at(b - 1, 8))
                    sp.dma_start(keys_t[:, :, :], ctx_t[b].rearrange("(k p) n -> p k n", p=P)).then_inc(
                        ct_ld.sem, 16)
                if att:
                    sp.wait_ge(consts.sem, 7)
                    sp.wait_ge(x1_copy.sem, x1_copy.at(i - 1, 1))
                    sp.dma_start(xn[:, :, :], x[i].rearrange("(m p) e -> p m e", p=P)).then_inc(xn_ld.sem, 16)
                if nxt:
                    sp.wait_ge(consts.sem, 7)
                    sp.wait_ge(k_lo.sem, k_lo.at(i - 1, 1))
                    sp.wait_ge(consts.sem, 7)
                    sp.wait_ge(xT_lo.sem, xT_lo.at(i, 1))
                    sp.dma_start(stage[:, :].rearrange("p (k n) -> p k n", k=KT),
                                 xT[i + 1].rearrange("(k p) n -> p k n", p=P)).then_inc(xT_ld.sem, 16)
                if cross:
                    for s in range(2):
                        sp.wait_ge(consts.sem, 7)
                        sp.wait_ge((nm_hi, nm_lo)[s].sem, (nm_hi, nm_lo)[s].at(b, 1))
                        sp.dma_start(Qst[96 + s:97 + s, :, :].rearrange("p h (t c) -> p (h t) c", c=P),
                                     nm[:, s, :]).then_inc(nm_st.sem, 16)
                if att:
                    if nxt:
                        sp.wait_ge(consts.sem, 7)
                        sp.wait_ge(xT_lo.sem, xT_lo.at(i + 1, 1))
                    else:
                        sp.wait_ge(consts.sem, 7)
                        sp.wait_ge(k_lo.sem, k_lo.at(i - 1, 1))
                    sp.dma_start(stage[:, :].rearrange("p (m e) -> p m e", m=MT),
                                 ctx_n[i].rearrange("(m p) e -> p m e", p=P)).then_inc(c_ld.sem, 16)
                    if cross:
                        sp.wait_ge(consts.sem, 7)
                        sp.wait_ge(s2_mm.sem, s2_mm.at(b, TILES))
                    for src, dst, order, done, rdy in ((hl, Qst, (0, 1, 0), q_st, q_lo),
                                                       (ksplit, Kst, (0, 0, 1), k_st, k_lo)):
                        sp.wait_ge(consts.sem, 7)
                        sp.wait_ge(rdy.sem, rdy.at(i, 1))
                        for j, s in enumerate(order):
                            for hd in range(HG):
                                sp.dma_start(
                                    dst[32 * j:32 * j + 32, :, :].rearrange("p (m v) e -> p v m e", v=HG)[:, hd],
                                    src[32 * hd:32 * hd + 32, s, :, :]).then_inc(done.sem, 16)
                if ffn:
                    sp.wait_ge(consts.sem, 7)
                    sp.wait_ge(out_rdy.sem, out_rdy.at(i - 2, 1))
                    sp.dma_start(out[i - 2].rearrange("(m p) e -> p m e", p=P), x2[:, :, :]).then_inc(
                        out_st.sem, 16)

            run_stages(sp, stages)
            sp.wait_ge(consts.sem, 7)
            sp.wait_ge(out_st.sem, out_st.at(B - 1, 1))

        @block.gpsimd
        def _(pool):
            g = nc.gpsimd
            g.memset(ones[:, :], 1.0).then_inc(consts.sem, 1)
            g.memset(mhalf[:, :], -0.5).then_inc(consts.sem, 1)
            g.memset(eps[:, :], EPS_LN).then_inc(consts.sem, 1)
            g.memset(id16[:, :], 0.0).then_inc(consts.sem, 1)
            g.memset(id32[:, :], 0.0).then_inc(consts.sem, 1)
            pool.wait_ge(consts.sem, consts.at(0, 5))
            for t in (id16, id32):
                g.affine_select(out=t[:, :], in_=t[:, :], compare_op=ALU.not_equal, fill=1.0, base=0,
                                pattern=[[-1, P]], channel_multiplier=1).then_inc(consts.sem, 1)

            def all_max(rdy, done, dst, src, b, k=1):
                pool.wait_ge(rdy.sem, rdy.at(b, k))
                if not isinstance(b, int):
                    g.tensor_tensor(pause_c if rdy is am_c_rdy else pause_x, mhalf[:, 0:1], mhalf[:, 0:1],
                                    ALU.add)
                g.partition_all_reduce(dst, src, P, RMAX).then_inc(done.sem, 1)

            def rstd_of(r, b):
                pool.wait_ge(ln_ag[r].sem, ln_ag[r].at(b, MT))
                g.tensor_tensor(ve[r][:, :], mv[r][:, :, 1], eps[:, :], ALU.add).then_inc(ln_ve[r].sem, 1)
                pool.wait_ge(ln_ve[r].sem, ln_ve[r].at(b, 1))
                g.tensor_tensor(rstd[r][:, :], ve[r][:, :], mhalf[:, :], ALU.pow).then_inc(ln_rs[r].sem, 1)

            all_max(am_w_rdy, amr_w_rdy, amr_w, am_w, 0, 1)
            all_max(am_x_rdy, amr_x_rdy, amr_x, am_x, 0)
            all_max(am_w_rdy, amr_w_rdy, amr_w, am_w, 0, 2)
            pool.wait_ge(small_ld.sem, small_ld.at(0, 2))

            def stages(i, att, cross, ffn, nxt):
                b = i - 1
                if att:
                    pool.wait_ge(xn_ld.sem, xn_ld.at(i, 1))
                    g.tensor_tensor(xn[:, :, :], xn[:, :, :],
                                    fcb_b[:, :].rearrange("p (a e) -> p a e", a=1).to_broadcast([P, MT, E]),
                                    ALU.add).then_inc(xb_rdy.sem, 1)

                def add_tiles(u):
                    lt, grp = u % KT, u // KT
                    for v in range(HG):
                        n = u * HG + v
                        pool.wait_ge(s2_exp.sem, s2_exp.at(b, n + 1))
                        if lt == 0:
                            if v == 0:
                                pool.wait_ge(den_mm.sem, den_mm.at(b, grp))
                            g.tensor_tensor(Psum[:, v, :], Pe[:, v, :], ones[:, 0:1].to_broadcast([P, E]),
                                            ALU.mult).then_inc(p_add.sem, 1)
                        else:
                            pool.wait_ge(p_add.sem, p_add.at(b, n - HG + 1))
                            g.tensor_tensor(Psum[:, v, :], Psum[:, v, :], Pe[:, v, :],
                                            ALU.add).then_inc(p_add.sem, 1)

                for u in range(8):
                    if u == 1 and att:
                        rstd_of(0, i)
                    if u == 2 and nxt:
                        all_max(am_x_rdy, amr_x_rdy, amr_x, am_x, i + 1)
                    if u == 5 and att:
                        all_max(am_c_rdy, amr_c_rdy, amr_c, am_c, i)
                    if cross:
                        add_tiles(u)
                if ffn:
                    rstd_of(2, i - 2)
                if cross:
                    rstd_of(1, b)

            run_stages(pool, stages)

        @block.scalar
        def _(act):
            a = nc.scalar

            def tiles_ab(first):
                for t in range(first, first + H * KT):
                    act.wait_ge(ab_mm.sem, ab_mm.at(0, t + 1))
                    if t == H * KT:
                        act.wait_ge(ab_lo.sem, ab_lo.at(0, 1))
                    a.activation(hold[:, (t - first) // KT, (t - first) % KT, :], L[t % 2][:, :],
                                 ACT.Copy).then_inc(ab_ev.sem, 1)

            def split_hi(dst, n):
                act.wait_ge(sw_rdy.sem, sw_rdy.at(0, n + 1))
                a.activation(dst[:, 0].rearrange("p h k e -> p (h k e)"), work_b[:, :], ACT.Copy,
                             scale=s_w).then_inc(ab_hi.sem, 1)

            def xT_split_hi(b):
                act.wait_ge(xs_step.sem, xs_step.at(b, 5))
                a.activation(xTs[:, 0].rearrange("p k n -> p (k n)"), stage[:, :], ACT.Copy,
                             scale=s_x).then_inc(xT_hi.sem, 1)

            tiles_ab(0)
            split_hi(A, 0)
            tiles_ab(H * KT)
            split_hi(Bm, 1)
            xT_split_hi(0)

            def stages(i, att, cross, ffn, nxt):
                b, f = i - 1, i - 2

                def weight_hi(h):
                    act.wait_ge(wsc_rdy.sem, wsc_rdy.at(i, h + 1))
                    for m in range(MT):
                        last = a.activation(ws[:, 0, h, m, :], we[:, h % 2, m, :], ACT.Copy,
                                            scale=r4[:, h, m:m + 1])
                    last.then_inc(w_hi.sem, 1)

                for j, (kind, h, m) in enumerate(BLOCKS):
                    if cross and j == 2:
                        act.wait_ge(q_lo.sem, q_lo.at(b, 1))
                        if ffn:
                            act.wait_ge(x2_rdy.sem, x2_rdy.at(f, 1))
                        a.activation(x1[:, :, :].rearrange("p m e -> p (m e)"),
                                     xn[:, :, :].rearrange("p m e -> p (m e)"), ACT.Copy).then_inc(x1_copy.sem, 1)
                    if att:
                        act.wait_ge(l_mm.sem, l_mm.at(i, j + 1))
                        if kind == "S":
                            act.wait_ge(bias_rdy.sem, bias_rdy.at(i, h + 1))
                            if h == 2:
                                act.wait_ge(w_lo.sem, w_lo.at(i, 1))
                            for mt in range(MT):
                                last = a.activation(we[:, h % 2, mt, :], L[j % 2][:, mt * N:mt * N + N], ACT.Exp,
                                                    bias=nb[:, h, mt:mt + 1], scale=esc,
                                                    accum_out=sm[:, h, mt:mt + 1])
                            last.then_inc(e_done.sem, 1)
                        else:
                            dst = (Gs[:, h % 2, 0, 2 * m:2 * m + 2, :].rearrange("p k n -> p (k n)")
                                   if kind == "G" else Vs[:, 0, h, m, :])
                            a.activation(dst, L[j % 2][:, :], ACT.Copy, scale=DOWN).then_inc(gv_hi.sem, 1)
                        if j - 1 in SB:
                            weight_hi(SB.index(j - 1))
                    if ffn and j == 3:
                        act.wait_ge(x2_rdy.sem, x2_rdy.at(f, 1))
                        act.wait_ge(q_st.sem, q_st.at(b, 3 * HG)) if cross else None
                        a.activation(hl[:, 0].rearrange("p m e -> p (m e)"),
                                     x2[:, :, :].rearrange("p m e -> p (m e)"), ACT.Copy,
                                     scale=X2S).then_inc(x2_hi.sem, 1)
                    if ffn and j in (7, 9):
                        s = (j - 7) // 2
                        act.wait_ge(xt_mm.sem, xt_mm.at(f, s + 1))
                        a.activation(x2T[:, s].rearrange("p k n -> p (k n)"), T16, ACT.Copy).then_inc(
                            xt_ev.sem, 1)

                def exps(u, v):
                    n = u * HG + v
                    act.wait_ge(s2_mm.sem, s2_mm.at(b, n + 1))
                    if n >= HG:
                        act.wait_ge(p_add.sem, p_add.at(b, n - HG + 1))
                    a.activation(Pe[:, v, :], S[n % 2][:, :], ACT.Exp, scale=xsc).then_inc(s2_exp.sem, 1)

                for u in range(8):
                    if cross:
                        if u == 0:
                            act.wait_ge(xsc_rdy.sem, xsc_rdy.at(b, 1))
                        exps(u, 0)
                        exps(u, 1)
                    if ffn:
                        act.wait_ge(u_mm.sem, u_mm.at(f, u + 1))
                        a.activation(th[:, u % 2, :], bank["U"][:, :], ACT.Tanh, scale=half_u).then_inc(
                            th_rdy.sem, 1)
                    if cross:
                        exps(u, 2)
                        exps(u, 3)
                    if ffn:
                        act.wait_ge(p_rdy.sem, p_rdy.at(f, u + 1))
                        a.activation(hs[:, u % 2, 0].rearrange("p e n -> p (e n)"), th[:, u % 2, :],
                                     ACT.Copy).then_inc(h_hi.sem, 1)
                    if u == 1 and att:
                        act.wait_ge(x1_rdy.sem, x1_rdy.at(i, 1))
                        if ffn:
                            act.wait_ge(xt_mm.sem, xt_mm.at(f, 2))
                        a.activation(hl[:, 0].rearrange("p m e -> p (m e)"),
                                     xn[:, :, :].rearrange("p m e -> p (m e)"), ACT.Copy,
                                     scale=QS).then_inc(q_hi.sem, 1)
                    if u == 3 and nxt:
                        xT_split_hi(i + 1)
                    if u == 6 and att:
                        act.wait_ge(cs_step.sem, cs_step.at(i, 3))
                        act.wait_ge(k_st.sem, k_st.at(i - 1, 3 * HG))
                        a.activation(ksplit[:, 0].rearrange("p m e -> p (m e)"), stage[:, :], ACT.Copy,
                                     scale=s_c).then_inc(k_hi.sem, 1)

            run_stages(act, stages)

        @block.tensor
        def _(pe):
            t_ = nc.tensor
            pe.wait_ge(consts.sem, consts.at(0, 7))
            for t in range(2 * H * KT):
                h, et = t // KT % H, t % KT
                if t < H * KT:
                    nl, nr = 2 * h, 2 * h + 1
                else:
                    nl, nr = 7 + h, 6
                if et == 0:
                    for n in (nl, nr):
                        pe.wait_ge(w_ld[SLOT[n]].sem, w_ld[SLOT[n]].at(0, SLOT[:n + 1].count(SLOT[n])))
                if t >= 2:
                    pe.wait_ge(ab_ev.sem, ab_ev.at(0, t - 1))
                lhs = ring_of(nl).rearrange("p (k e) -> p k e", k=KT)
                rhs = ring_of(nr).rearrange("p (k e) -> p k e", k=KT)
                for k in range(KT):
                    last = t_.matmul(L[t % 2][:, :], lhs[:, k, et * P:(et + 1) * P], rhs[:, k, :],
                                     start=(k == 0), stop=(k == KT - 1))
                last.then_inc(ab_mm.sem, 1)
                if t in (H * KT - 1, H * KT + 5, 2 * H * KT - 1):
                    m = (H * KT - 1, H * KT + 5, 2 * H * KT - 1).index(t)
                    pe.wait_ge(f_tot.sem, f_tot.at(0, m + 1))
                    t_.matmul(bank["U"][:, m:m + 1], ones[:, :], tot[:, m:m + 1], start=True,
                              stop=True).then_inc(f_mm.sem, 1)

            def split_products(dst, terms):
                for n, (lhs, rhs) in enumerate(terms):
                    last = t_.matmul(dst, lhs, rhs, start=(n == 0), stop=(n == len(terms) - 1))
                return last

            PARTS = ((0, 0), (0, 1), (1, 0))

            def stages(i, att, cross, ffn, nxt):
                b, f = i - 1, i - 2

                def s1(t):
                    h, qt = t // KT, t % KT
                    if t == 0:
                        pe.wait_ge(q_st.sem, q_st.at(b, 3 * HG))
                        pe.wait_ge(k_st.sem, k_st.at(b, 3 * HG))
                    if t >= 2:
                        pe.wait_ge(s1_max.sem, s1_max.at(b, t - 1))
                    t_.matmul(S[t % 2][:, :], Qst[0:96, h, qt * P:(qt + 1) * P], Kst[0:96, h, :], start=True,
                              stop=True).then_inc(s1_mm.sem, 1)

                for j, (kind, h, m) in enumerate(BLOCKS):
                    pend = list(s1_of.get(j, ())) if cross else []

                    def s1_next():
                        if pend:
                            s1(pend.pop(0))

                    if att:
                        bk = L[j % 2]
                        if j == 0:
                            pe.wait_ge(xT_lo.sem, xT_lo.at(i, 1))
                            if isinstance(i, int) and i == 0:
                                pe.wait_ge(ab_lo.sem, ab_lo.at(0, 2))
                        if j < 2:
                            if ffn:
                                pe.wait_ge(y3_rdy.sem, y3_rdy.at(f - 1, MT))
                            pe.wait_ge(y1_rdy.sem, y1_rdy.at(i - 1, MT))
                        elif (j - 2) in SB:
                            pe.wait_ge(e_done.sem, e_done.at(i, SB.index(j - 2) + 1))
                        else:
                            pe.wait_ge(gv_lo.sem, gv_lo.at(i, GV.index(j - 2) + 1))
                        if kind == "G":
                            for c in range(2):
                                cols = slice((2 * m + c) * P, (2 * m + c + 1) * P)
                                last = split_products(bk[:, c * N:(c + 1) * N], [
                                    (A[:, pl, h, k, cols], xTs[:, pr, k, :]) for pl, pr in PARTS for k in range(KT)])
                                s1_next()
                        elif kind == "S":
                            pe.wait_ge(gv_lo.sem, gv_lo.at(i, GV.index(BLOCKS.index(("G", h, 1))) + 1))
                            for c in range(MT):
                                last = split_products(bk[:, c * N:(c + 1) * N], [
                                    (xTs[:, pl, k, c * P:(c + 1) * P], Gs[:, h % 2, pr, k, :])
                                    for pl, pr in PARTS for k in range(KT)])
                                s1_next()
                        else:
                            last = split_products(bk[:, :], [
                                (xTs[:, pl, k, m * P:(m + 1) * P], Bm[:, pr, h, k, :])
                                for pl, pr in PARTS for k in range(KT)])
                        last.then_inc(l_mm.sem, 1)
                    while pend:
                        s1_next()
                    if ffn and j in (5, 8):
                        s = (j - 5) // 3
                        pe.wait_ge((x2_hi, x2_lo)[s].sem, (x2_hi, x2_lo)[s].at(f, 1))
                        if s == 0:
                            pe.wait_ge(den_inv.sem, den_inv.at(b - 1, MT))
                        else:
                            pe.wait_ge(xt_ev.sem, xt_ev.at(f, 1))
                        for k in range(KT):
                            for mt in range(MT):
                                c0 = k * N + mt * P
                                last = t_.transpose(T16[:, c0:c0 + P], hl[:, s, mt, k * P:(k + 1) * P], id16[:, :])
                        last.then_inc(xt_mm.sem, 1)
                if cross:
                    pe.wait_ge(s1_max.sem, s1_max.at(b, TILES))
                    if ffn:
                        pe.wait_ge(xt_ev.sem, xt_ev.at(f, 2))
                    pe.wait_ge(den_inv.sem, den_inv.at(b - 1, MT))
                    t_.transpose(bank["T"][0:TILES, 0:P], xmx[:, :], id32[:, :]).then_inc(nt_mm.sem, 1)
                if att:
                    pe.wait_ge(w_lo.sem, w_lo.at(i, H))
                    pe.wait_ge(gv_lo.sem, gv_lo.at(i, NGV))
                    for n in range(MT):
                        j = NBLK + n
                        split_products(L[j % 2][:, :], [
                            (ws[:, pl, h, m, n * P:(n + 1) * P], Vs[:, pr, h, m, :])
                            for h in range(H) for m in range(MT) for pl, pr in PARTS]).then_inc(l_mm.sem, 1)

                def s2(u, v):
                    n = u * HG + v
                    h, lt = HG * (u // KT) + v, u % KT
                    if n == 0:
                        pe.wait_ge(nm_st.sem, nm_st.at(b, 2))
                        pe.wait_ge(krow.sem, krow.at(0, 1))
                    if n >= 2:
                        pe.wait_ge(s2_exp.sem, s2_exp.at(b, n - 1))
                    t_.matmul(S[n % 2][:, :], Kst[0:98, h, lt * P:(lt + 1) * P], Qst[0:98, h, :], start=True,
                              stop=True).then_inc(s2_mm.sem, 1)

                def hidden(u, W, dst, done, free):
                    for e in range(2):
                        if ffn:
                            if e == 0:
                                pe.wait_ge(free.sem, free.at(f, u))
                            cols = slice((2 * u + e) * P, (2 * u + e + 1) * P)
                            last = split_products(dst[:, e * N:(e + 1) * N], [
                                (W[:, k, cols], x2T[:, s, k, :]) for s in range(2) for k in range(KT)])
                            if e == 1:
                                last.then_inc(done.sem, 1)
                        if cross:
                            s2(u, 2 * (dst is bank["G"]) + e)

                def down(u):
                    pe.wait_ge(h_lo.sem, h_lo.at(f, u + 1))
                    if u == 0:
                        if att:
                            pe.wait_ge(y1_rdy.sem, y1_rdy.at(i, MT))
                        pe.wait_ge(y3_rdy.sem, y3_rdy.at(f - 1, MT))
                    for n in range(MT):
                        for e in range(2):
                            for s in range(2):
                                last = t_.matmul(L[n][:, :], hs[:, u % 2, s, e, n * P:(n + 1) * P],
                                                 Wd[:, 2 * u + e, :], start=(u == 0 and e == 0 and s == 0),
                                                 stop=(u == PAIRS - 1 and e == 1 and s == 1))
                    last.then_inc(dn_mm.sem, 1)

                def pv(u):
                    grp, lt = u // KT, u % KT
                    if u == 0:
                        pe.wait_ge(ct_ld.sem, ct_ld.at(b, 1))
                    if lt == 0:
                        pe.wait_ge(o_read.sem, o_read.at(b, grp))
                    pe.wait_ge(s2_exp.sem, s2_exp.at(b, HG * (u + 1)))
                    for v in range(HG):
                        c0 = grp * P + v * DH
                        last = t_.matmul(bank["O"][v * DH:(v + 1) * DH, :], keys_t[:, lt, c0:c0 + DH], Pe[:, v, :],
                                         start=(lt == 0), stop=(lt == KT - 1), skip_group_check=True)
                    last.then_inc(pv_mm.sem, 1)

                def denom(grp):
                    pe.wait_ge(p_add.sem, p_add.at(b, (grp + 1) * KT * HG))
                    (pe.wait_ge(den_inv.sem, den_inv.at(b, 1)) if grp else pe.wait_ge(nm_lo.sem, nm_lo.at(b, 1)))
                    for v in range(HG):
                        last = t_.matmul(bank["T"][v * DH:(v + 1) * DH, :], ones[:, 0:DH], Psum[:, v, :],
                                         start=True, stop=True, skip_group_check=True)
                    last.then_inc(den_mm.sem, 1)

                if ffn:
                    pe.wait_ge(xt_ev.sem, xt_ev.at(f, 2))
                for u in range(8):
                    hidden(u, Wu, bank["U"], u_mm, t_rdy)
                    if u == 4 and cross:
                        denom(0)
                    hidden(u, Wg, bank["G"], g_mm, p_rdy)
                    if ffn and u:
                        down(u - 1)
                    if cross:
                        pv(u)
                if ffn:
                    down(PAIRS - 1)
                if cross:
                    denom(1)

            run_stages(pe, stages)

        @block.vector
        def _(dve):
            v_ = nc.vector
            steps = [0]

            def step(ins):
                steps[0] += 1
                ins.then_inc(prep.sem, 1)
                dve.wait_ge(prep.sem, prep.at(0, steps[0]))

            def x_absmax(b):
                dve.wait_ge(xT_ld.sem, xT_ld.at(b, 1))
                v_.tensor_reduce(am_x, stage[:, :], AXX, ALU.max, apply_absolute_value=True).then_inc(
                    am_x_rdy.sem, 1)

            def x_scales(b):
                dve.wait_ge(amr_x_rdy.sem, amr_x_rdy.at(b, 1))
                v_.tensor_scalar(amr_x, amr_x, 1e-30, None, ALU.max).then_inc(xs_step.sem, 1)
                dve.wait_ge(xs_step.sem, xs_step.at(b, 1))
                v_.reciprocal(inv_x, amr_x).then_inc(xs_step.sem, 1)
                v_.scalar_tensor_tensor(esc, amr_x, amr_x, c_esc, ALU.mult, ALU.mult).then_inc(xs_step.sem, 1)
                v_.tensor_tensor(asc, amr_x, c_asc, ALU.mult).then_inc(xs_step.sem, 1)
                dve.wait_ge(xs_step.sem, xs_step.at(b, 2))
                v_.tensor_scalar(s_x, inv_x, TOP, None, ALU.mult).then_inc(xs_step.sem, 1)

            def x_lo(b):
                dve.wait_ge(xT_hi.sem, xT_hi.at(b, 1))
                v_.scalar_tensor_tensor(xTs[:, 1].rearrange("p k n -> p (k n)"), stage[:, :], s_x,
                                        xTs[:, 0].rearrange("p k n -> p (k n)"), ALU.mult,
                                        ALU.subtract).then_inc(xT_lo.sem, 1)

            def matrix_scale(n, back, const):
                dve.wait_ge(ab_ev.sem, ab_ev.at(0, (n + 1) * H * KT))
                v_.tensor_reduce(am_w, work_b[:, :], AXX, ALU.max, apply_absolute_value=True).then_inc(
                    am_w_rdy.sem, 1)
                dve.wait_ge(amr_w_rdy.sem, amr_w_rdy.at(0, n + 1))
                step(v_.tensor_scalar(amr_w, amr_w, 1e-30, None, ALU.max))
                step(v_.reciprocal(inv_w, amr_w))
                step(v_.tensor_scalar(back, amr_w, const, None, ALU.mult))
                v_.tensor_scalar(s_w, inv_w, TOP, None, ALU.mult).then_inc(sw_rdy.sem, 1)

            def matrix_lo(dst, n):
                dve.wait_ge(ab_hi.sem, ab_hi.at(0, n + 1))
                v_.scalar_tensor_tensor(dst[:, 1].rearrange("p h k e -> p (h k e)"), work_b[:, :], s_w,
                                        dst[:, 0].rearrange("p h k e -> p (h k e)"), ALU.mult,
                                        ALU.subtract).then_inc(ab_lo.sem, 1)

            def ternary(m):
                for c in range(4):
                    dve.wait_ge(f_ld[c].sem, f_ld[c].at(0, m + 1))
                    last = v_.tensor_reduce(part[:, m, 4 * c:4 * c + 4],
                                            stg[:, c, :].rearrange("p (q e) -> p q e", e=E), AXX, ALU.add,
                                            apply_absolute_value=True)
                step(last)
                v_.tensor_reduce(tot[:, m:m + 1], part[:, m, :], AXX, ALU.add).then_inc(f_tot.sem, 1)
                dve.wait_ge(f_mm.sem, f_mm.at(0, m + 1))
                step(v_.tensor_scalar(mean_w[:, m:m + 1], bank["U"][:, m:m + 1], 1.0 / (E * F), EPS_Q, ALU.mult,
                                      ALU.add))
                step(v_.tensor_scalar(thr[:, m:m + 1], mean_w[:, m:m + 1], 0.5, None, ALU.mult))
                step(v_.tensor_scalar(nthr[:, m:m + 1], mean_w[:, m:m + 1], -0.5, None, ALU.mult))
                W = [Wu, Wg, Wd][m]
                for c in range(4):
                    dst = W[:, c, :] if m < 2 else W[:, 4 * c:4 * c + 4, :].rearrange("p k e -> p (k e)")
                    step(v_.tensor_scalar(dst, stg[:, c, :], nthr[:, m:m + 1], None, ALU.is_lt))
                    v_.scalar_tensor_tensor(dst, stg[:, c, :], thr[:, m:m + 1], dst, ALU.is_gt,
                                            ALU.subtract).then_inc(quant.sem, 1)

            def ln_stats(r, b, src):
                for m in range(MT):
                    v_.bn_stats(bst[r][:, m, :], src[:, m, :]).then_inc(ln_st[r].sem, 1)
                dve.wait_ge(ln_st[r].sem, ln_st[r].at(b, MT))
                v_.memset(pause, 0.0)
                for m in range(MT):
                    v_.bn_aggr(mv[r][:, m, :], bst[r][:, m, :]).then_inc(ln_ag[r].sem, 1)

            def ln_apply(r, b, dst, src):
                dve.wait_ge(ln_rs[r].sem, ln_rs[r].at(b, 1))
                for m in range(MT):
                    last = v_.tensor_scalar(dst[:, m, :], src[:, m, :], mv[r][:, m, 0:1], rstd[r][:, m:m + 1],
                                            ALU.subtract, ALU.mult)
                return last

            ternary(0)
            matrix_scale(0, c_esc, ESC)
            x_absmax(0)
            matrix_lo(A, 0)
            ternary(1)
            matrix_scale(1, c_asc, ASC)
            matrix_lo(Bm, 1)
            x_scales(0)
            x_lo(0)
            ternary(2)
            v_.memset(Kst[96:98, :, :], MROW).then_inc(krow.sem, 1)
            step(v_.tensor_scalar(half_u, mean_w[:, 0:1], 0.5 / X2S, None, ALU.mult))
            step(v_.tensor_tensor(gd, mean_w[:, 1:2], mean_w[:, 2:3], ALU.mult))
            step(v_.tensor_scalar(gd, gd, mean_w[:, 0:1], DSC, ALU.mult, ALU.mult))
            dve.wait_ge(small_ld.sem, small_ld.at(0, 2))

            def stages(i, att, cross, ffn, nxt):
                b, f = i - 1, i - 2

                def weight_scale(h):
                    dve.wait_ge(e_done.sem, e_done.at(i, h + 1))
                    v_.reciprocal(rs[:, h, :], sm[:, h, :]).then_inc(sum_inv.sem, 1)
                    dve.wait_ge(sum_inv.sem, sum_inv.at(i, h + 1))
                    v_.tensor_scalar(r4[:, h, :], rs[:, h, :], WTOP, None, ALU.mult).then_inc(wsc_rdy.sem, 1)

                def weight_lo(h):
                    dve.wait_ge(w_hi.sem, w_hi.at(i, h + 1))
                    for m in range(MT):
                        last = v_.scalar_tensor_tensor(ws[:, 1, h, m, :], we[:, h % 2, m, :], r4[:, h, m:m + 1],
                                                       ws[:, 0, h, m, :], ALU.mult, ALU.subtract)
                    last.then_inc(w_lo.sem, 1)

                if cross:
                    v_.tensor_scalar(xsc, amr_c, XSC, None, ALU.mult).then_inc(xsc_rdy.sem, 1)
                for j, (kind, h, m) in enumerate(BLOCKS):
                    if att:
                        bk = L[j % 2]
                        if kind == "S":
                            dve.wait_ge(l_mm.sem, l_mm.at(i, j + 1))
                            v_.tensor_reduce(cm[:, h, :], bk[:, :].rearrange("p (m n) -> p m n", m=MT), AXX,
                                             ALU.max).then_inc(cmax.sem, 1)
                            dve.wait_ge(cmax.sem, cmax.at(i, h + 1))
                            v_.tensor_scalar(nb[:, h, :], cm[:, h, :], esc, -1.0, ALU.mult,
                                             ALU.mult).then_inc(bias_rdy.sem, 1)
                        else:
                            dve.wait_ge(gv_hi.sem, gv_hi.at(i, GV.index(j) + 1))
                            hi, lo = ([Gs[:, h % 2, s, 2 * m:2 * m + 2, :].rearrange("p k n -> p (k n)")
                                       for s in range(2)] if kind == "G" else [Vs[:, s, h, m, :] for s in range(2)])
                            v_.scalar_tensor_tensor(lo, bk[:, :], DOWN, hi, ALU.mult,
                                                    ALU.subtract).then_inc(gv_lo.sem, 1)
                        if j - 1 in SB:
                            weight_scale(SB.index(j - 1))
                        if j - 2 in SB:
                            weight_lo(SB.index(j - 2))
                    if cross:
                        for t in s1_of.get(j, ()):
                            dve.wait_ge(s1_mm.sem, s1_mm.at(b, t + 1))
                            v_.tensor_reduce(xmx[:, t:t + 1], S[t % 2][:, :], AXX, ALU.max).then_inc(
                                s1_max.sem, 1)
                    if ffn and j == 1:
                        dve.wait_ge(out_st.sem, out_st.at(f - 1, 1))
                        ln_apply(1, f, x2, x1).then_inc(x2_rdy.sem, 1)
                    if ffn and j == 4:
                        dve.wait_ge(x2_hi.sem, x2_hi.at(f, 1))
                        v_.scalar_tensor_tensor(hl[:, 1], x2[:, :, :], X2S, hl[:, 0], ALU.mult,
                                                ALU.subtract).then_inc(x2_lo.sem, 1)
                if cross:
                    dve.wait_ge(nt_mm.sem, nt_mm.at(b, 1))
                    dve.wait_ge(nm_st.sem, nm_st.at(b - 1, 2))
                    v_.tensor_scalar(nm[:, 0, :], bank["T"][0:TILES, 0:P], -1.0 / MROW, None,
                                     ALU.mult).then_inc(nm_hi.sem, 1)
                    dve.wait_ge(nm_hi.sem, nm_hi.at(b, 1))
                    v_.scalar_tensor_tensor(nm[:, 1, :], bank["T"][0:TILES, 0:P], -1.0 / MROW, nm[:, 0, :],
                                            ALU.mult, ALU.subtract).then_inc(nm_lo.sem, 1)
                if att:
                    dve.wait_ge(xb_rdy.sem, xb_rdy.at(i, 1))
                    for n in range(MT):
                        dve.wait_ge(l_mm.sem, l_mm.at(i, NBLK + n + 1))
                        v_.scalar_tensor_tensor(xn[:, n, :], L[(NBLK + n) % 2][:, :], asc, xn[:, n, :], ALU.mult,
                                                ALU.add).then_inc(y1_rdy.sem, 1)
                    dve.wait_ge(y1_rdy.sem, y1_rdy.at(i, MT))
                    ln_stats(0, i, xn)

                def pair_t(u):
                    dve.wait_ge(th_rdy.sem, th_rdy.at(f, u + 1))
                    v_.scalar_tensor_tensor(th[:, u % 2, :], th[:, u % 2, :], 1.0, bank["U"][:, :], ALU.add,
                                            ALU.mult).then_inc(t_rdy.sem, 1)

                def pair_p(u):
                    dve.wait_ge(g_mm.sem, g_mm.at(f, u + 1))
                    dve.wait_ge(t_rdy.sem, t_rdy.at(f, u + 1))
                    v_.scalar_tensor_tensor(th[:, u % 2, :], th[:, u % 2, :], HS / 2, bank["G"][:, :], ALU.mult,
                                            ALU.mult).then_inc(p_rdy.sem, 1)

                def pair_lo(u):
                    dve.wait_ge(h_hi.sem, h_hi.at(f, u + 1))
                    v_.tensor_tensor(hs[:, u % 2, 1].rearrange("p e n -> p (e n)"), th[:, u % 2, :],
                                     hs[:, u % 2, 0].rearrange("p e n -> p (e n)"),
                                     ALU.subtract).then_inc(h_lo.sem, 1)

                def cross_out(grp):
                    dve.wait_ge(den_mm.sem, den_mm.at(b, grp + 1))
                    v_.reciprocal(den[:, :], bank["T"][:, :]).then_inc(den_inv.sem, 1)
                    dve.wait_ge(den_inv.sem, den_inv.at(b, grp + 1))
                    dve.wait_ge(pv_mm.sem, pv_mm.at(b, KT * (grp + 1)))
                    v_.tensor_tensor(den[:, :], bank["O"][:, :], den[:, :], ALU.mult).then_inc(o_read.sem, 1)
                    dve.wait_ge(o_read.sem, o_read.at(b, grp + 1))
                    if grp == 0:
                        dve.wait_ge(x1_copy.sem, x1_copy.at(b, 1))
                    v_.scalar_tensor_tensor(x1[:, grp, :], den[:, :], gam[:, 0:1], x1[:, grp, :], ALU.mult,
                                            ALU.add).then_inc(y2_rdy.sem, 1)

                for u in range(8):
                    if ffn:
                        pair_t(u)
                    if u == 4 and cross:
                        cross_out(0)
                    if u == 1 and att:
                        ln_apply(0, i, xn, xn).then_inc(x1_rdy.sem, 1)
                    if u == 1 and nxt:
                        x_absmax(i + 1)
                    if u == 2 and att:
                        dve.wait_ge(q_hi.sem, q_hi.at(i, 1))
                        v_.scalar_tensor_tensor(hl[:, 1], xn[:, :, :], QS, hl[:, 0], ALU.mult,
                                                ALU.subtract).then_inc(q_lo.sem, 1)
                    if u == 3 and nxt:
                        x_scales(i + 1)
                    if u == 4 and nxt:
                        x_lo(i + 1)
                    if u == 5 and att:
                        dve.wait_ge(c_ld.sem, c_ld.at(i, 1))
                        v_.tensor_reduce(am_c, stage[:, :], AXX, ALU.max, apply_absolute_value=True).then_inc(
                            am_c_rdy.sem, 1)
                    if u == 6 and att:
                        dve.wait_ge(amr_c_rdy.sem, amr_c_rdy.at(i, 1))
                        v_.tensor_scalar(amr_c, amr_c, 1e-30, None, ALU.max).then_inc(cs_step.sem, 1)
                        dve.wait_ge(cs_step.sem, cs_step.at(i, 1))
                        v_.reciprocal(inv_c, amr_c).then_inc(cs_step.sem, 1)
                        dve.wait_ge(cs_step.sem, cs_step.at(i, 2))
                        v_.tensor_scalar(s_c, inv_c, KTOP, None, ALU.mult).then_inc(cs_step.sem, 1)
                    if ffn:
                        pair_p(u)
                        pair_lo(u)
                    if u == 7 and att:
                        dve.wait_ge(k_hi.sem, k_hi.at(i, 1))
                        v_.scalar_tensor_tensor(ksplit[:, 1].rearrange("p m e -> p (m e)"), stage[:, :], s_c,
                                                ksplit[:, 0].rearrange("p m e -> p (m e)"), ALU.mult,
                                                ALU.subtract).then_inc(k_lo.sem, 1)
                if ffn:
                    dve.wait_ge(dn_mm.sem, dn_mm.at(f, PAIRS))
                    for n in range(MT):
                        v_.scalar_tensor_tensor(x2[:, n, :], L[n][:, :], gd, x2[:, n, :], ALU.mult,
                                                ALU.add).then_inc(y3_rdy.sem, 1)
                if cross:
                    cross_out(1)
                if ffn:
                    dve.wait_ge(y3_rdy.sem, y3_rdy.at(f, MT))
                    ln_stats(2, f, x2)
                if cross:
                    dve.wait_ge(y2_rdy.sem, y2_rdy.at(b, MT))
                    ln_stats(1, b, x1)
                if ffn:
                    ln_apply(2, f, x2, x2).then_inc(out_rdy.sem, 1)

            run_stages(dve, stages)


def kernel(x, ctx_2048, L0_attn_Wq, L0_attn_Wk, L0_attn_Wv, L0_attn_fc_w, L0_attn_fc_b, L0_xattn_gamma,
           L0_ffn_W_up, L0_ffn_W_gate, L0_ffn_W_down):
    import numpy as np
    import concourse.bacc as bacc
    from concourse.bass_utils import run_bass_kernel_spmd

    c = np.ascontiguousarray
    arrays = {
        "x": c(x), "xT": c(np.transpose(x, (0, 2, 1))),
        "ctx_n": c(ctx_2048), "ctx_t": c(np.transpose(ctx_2048, (0, 2, 1))),
        "wq": c(L0_attn_Wq), "wk": c(L0_attn_Wk), "wv": c(L0_attn_Wv),
        "fcT": c(np.transpose(L0_attn_fc_w)), "fcb": c(L0_attn_fc_b),
        "gamma": c(np.reshape(L0_xattn_gamma, (1,))),
        "wu": c(np.transpose(L0_ffn_W_up)), "wg": c(np.transpose(L0_ffn_W_gate)),
        "wd": c(np.transpose(L0_ffn_W_down)),
    }
    nc = bacc.Bacc("TRN2", target_bir_lowering=False, num_devices=1)
    args = [nc.dram_tensor("in_" + n, a.shape, mybir.dt.from_np(a.dtype), kind="ExternalInput").ap()
            for n, a in arrays.items()]
    result = nc.dram_tensor("result", x.shape, F32, kind="ExternalOutput").ap()
    decoder_layer(nc, *args, result)
    r = run_bass_kernel_spmd(nc, [{"in_" + n: a for n, a in arrays.items()}], core_ids=[0])
    return r.results[0]["result"]
```

```python
from contextlib import ExitStack

import concourse.bass as bass
from concourse import mybir

F32 = mybir.dt.float32
F16 = mybir.dt.float16
ACT = mybir.ActivationFunctionType
ALU = mybir.AluOpType
AXX = mybir.AxisListType.X
RMAX = bass.bass_isa.ReduceOp.max

P = 128
EPS_LN = 1e-5
EPS_Q = 1e-8


class Signal:

    def __init__(self, sem, per, by=1):
        self.sem, self.per, self.by = sem, per, by

    def at(self, batch, count):
        return (batch * self.per + count) * self.by


def decoder_layer(nc, x, xT, ctx_n, ctx_t, wq, wk, wv, fcT, fcb, gamma, wu, wg, wd, out):
    B, N, E = x.shape
    H = wq.shape[0]
    F = wu.shape[1]
    KT = E // P
    MT = N // P
    DH = 32
    XH = N // DH
    HG = P // DH
    FT = F // P
    PAIRS = FT // 2
    assert (E, N, XH, PAIRS, H, MT, KT) == (512, 256, 8, 8, 3, 2, 4)

    TOP = 1024.0
    DOWN = 2.0 ** -14
    WTOP = 4096.0
    QS = 64.0
    KTOP = 4096.0
    MROW = 4096.0
    X2S = 32.0
    HS = 2.0 ** -13
    ESC = 1.0 / (DOWN * TOP ** 3 * E ** 0.5)
    ASC = 1.0 / (DOWN * WTOP * H * TOP ** 2)
    XSC = 1.0 / (QS * KTOP * DH ** 0.5)
    DSC = 1.0 / (HS * X2S * X2S)

    BLOCKS = [("G", 0, 0), ("G", 0, 1), ("G", 1, 0), ("G", 1, 1), ("S", 0, 0), ("G", 2, 0), ("G", 2, 1),
              ("S", 1, 0), ("S", 2, 0)] + [("V", h, m) for h in range(H) for m in range(MT)]
    GV = [j for j, b in enumerate(BLOCKS) if b[0] != "S"]
    SB = [j for j, b in enumerate(BLOCKS) if b[0] == "S"]
    NBLK = len(BLOCKS)
    NGV = len(GV)
    TILES = XH * KT
    GT = TILES // MT
    S1_TURN = 12
    s1_of = {j: range(GT * j // S1_TURN, GT * (j + 1) // S1_TURN) if j < S1_TURN
             else range(*((0, 0) if j == S1_TURN else (GT + 2 * (j - S1_TURN) - 2, GT + 2 * (j - S1_TURN))))
             for j in range(NBLK)}
    S1_BLOCKS = s1_of[NBLK - 1].stop
    S1_SLOTS = (TILES - S1_BLOCKS) // HG
    assert S1_BLOCKS + HG * S1_SLOTS == TILES and S1_SLOTS < KT

    with ExitStack() as ctx:
        def sb(name, shape, dt):
            return ctx.enter_context(nc.sbuf_tensor(name, shape, dt))

        def signal(name, per, by=1):
            return Signal(ctx.enter_context(nc.semaphore(name)), per, by)

        bank = {n: ctx.enter_context(nc.psum_tensor("bank_" + n, [P, 512], F32))
                for n in ("L0", "L1", "S0", "S1", "U", "G", "O", "T")}
        L = [bank["L0"], bank["L1"]]
        S = [bank["S0"], bank["S1"]]
        T16 = bank["T"][:, :].bitcast(F16)

        A = sb("score_matrix", [P, 2, H, KT, E], F16)
        Bm = sb("value_matrix", [P, 2, H, KT, E], F16)
        Wu = sb("ternary_up", [P, KT, F], F16)
        Wg = sb("ternary_gate", [P, KT, F], F16)
        Wd = sb("ternary_down", [P, FT, E], F16)
        stage = sb("stage", [P, 1024], F32)
        xTs = sb("xT_split", [P, 2, KT, N], F16)
        xn = sb("x_rows", [P, MT, E], F32)
        work_a = sb("work_a", [P, 6144], F32)
        work_b = sb("work_b", [P, 6144], F32)
        work_c = sb("work_c", [P, 8192], F32)
        keys_t = sb("ctx_columns", [P, KT, N], F32)
        ksplit = sb("key_split", [P, 2, MT, E], F16)
        Gs = work_a[:, 0:2048].bitcast(F16).rearrange("p (b s k n) -> p b s k n", b=2, s=2, k=KT)
        Vs = work_a[:, 2048:5120].bitcast(F16).rearrange("p (s h m e) -> p s h m e", s=2, h=H, m=MT)
        we = work_a[:, 5120:6144].rearrange("p (b m n) -> p b m n", b=2, m=MT)
        den = work_a[:, 5120:5632]
        x1 = work_b[:, 0:1024].rearrange("p (m e) -> p m e", m=MT)
        hl = work_b[:, 1024:2048].bitcast(F16).rearrange("p (s m e) -> p s m e", s=2, m=MT)
        Qst = work_b[:, 2048:4096].bitcast(F16).rearrange("p (h e) -> p h e", h=XH)
        Kst = work_b[:, 4096:6144].bitcast(F16).rearrange("p (h e) -> p h e", h=XH)
        Pe = work_c[:, 0:2048].rearrange("p (v e) -> p v e", v=HG)
        Psum = work_c[:, 2048:4096].rearrange("p (v e) -> p v e", v=HG)
        x2 = work_c[:, 4096:5120].rearrange("p (m e) -> p m e", m=MT)
        x2T = work_c[:, 5120:6144].bitcast(F16).rearrange("p (s k n) -> p s k n", s=2, k=KT)
        hs = work_c[:, 6144:7168].bitcast(F16).rearrange("p (b s e n) -> p b s e n", b=2, s=2, e=2)
        th = work_c[:, 7168:8192].rearrange("p (b e) -> p b e", b=2)
        ws = sb("weight_split", [P, 2, H, MT, N], F16)
        fcb_b = sb("fcb_b", [P, E], F32)
        gam = sb("gam", [P, 1], F32)
        ones = sb("ones", [P, P], F32)
        id16 = sb("id16", [P, P], F16)
        id32 = sb("id32", [P, P], F32)
        mhalf = sb("mhalf", [P, MT], F32)
        eps = sb("eps", [P, MT], F32)
        nm = sb("neg_max_rows", [GT, MT, 2, P], F16)
        xmx = sb("cross_max", [P, TILES], F32)
        cm = sb("col_max", [P, H, MT], F32)
        nb = sb("exp_bias", [P, H, MT], F32)
        sm = sb("exp_sum", [P, H, MT], F32)
        rs = sb("exp_sum_inv", [P, H, MT], F32)
        r4 = sb("weight_scale", [P, H, MT], F32)
        bst = [sb(f"bn{r}", [P, MT, 6], F32) for r in range(3)]
        mv = [sb(f"mean_var{r}", [P, MT, 2], F32) for r in range(3)]
        ve = [sb(f"var_eps{r}", [P, MT], F32) for r in range(3)]
        rstd = [sb(f"rstd{r}", [P, MT], F32) for r in range(3)]
        sc = sb("scales", [P, 24], F32)
        (am_x, amr_x, inv_x, s_x, sq_x, esc, asc, am_c, amr_c, inv_c, s_c, xsc, c_esc, c_asc, am_w, amr_w,
         inv_w, s_w) = (sc[:, n:n + 1] for n in range(18))
        part = sb("abs_parts", [P, 3, 16], F32)
        tot = sb("abs_total", [P, 3], F32)
        mean_w = sb("weight_mean", [P, 3], F32)
        thr = sb("threshold", [P, 3], F32)
        nthr = sb("neg_threshold", [P, 3], F32)
        fsc = sb("ffn_scales", [P, 4], F32)
        half_u, gd, dsc = (fsc[:, n:n + 1] for n in range(3))

        ring = [work_a[:, 0:2048], work_a[:, 2048:4096], work_a[:, 4096:6144]]
        hold = work_b[:, :].rearrange("p (h k e) -> p h k e", h=H, k=KT)
        stg = work_c[:, :].rearrange("p (c f) -> p c f", c=4)

        consts = signal("consts", 0)
        small_ld = signal("small_ld", 0, 16)
        w_ld = [signal(f"w_ld{n}", 0, 16) for n in range(3)]
        ab_mm = signal("ab_mm", 0)
        ab_ev = signal("ab_ev", 0)
        f_ld = [signal(f"f_ld{n}", 0, 16) for n in range(4)]
        f_abs = signal("f_abs", 0)
        f_tot = signal("f_tot", 0)
        f_mm = signal("f_mm", 0)
        prep = signal("prep", 0)
        am_w_rdy = signal("am_w_rdy", 0)
        amr_w_rdy = signal("amr_w_rdy", 0)
        sw_rdy = signal("sw_rdy", 0)
        ab_hi = signal("ab_hi", 0)
        ab_lo = signal("ab_lo", 0)
        quant = signal("quant", 0)
        krow = signal("krow", 0)
        xT_ld = signal("xT_ld", 1, 16)
        am_x_rdy = signal("am_x_rdy", 1)
        amr_x_rdy = signal("amr_x_rdy", 1)
        xs_step = signal("xs_step", 5)
        xT_hi = signal("xT_hi", 1)
        xT_lo = signal("xT_lo", 1)
        xn_ld = signal("xn_ld", 1, 16)
        xb_rdy = signal("xb_rdy", 1)
        l_mm = signal("l_mm", NBLK + MT)
        gv_hi = signal("gv_hi", NGV)
        gv_lo = signal("gv_lo", NGV)
        cmax = signal("cmax", H)
        bias_rdy = signal("bias_rdy", H)
        e_done = signal("e_done", H)
        sum_inv = signal("sum_inv", H)
        wsc_rdy = signal("wsc_rdy", H)
        w_hi = signal("w_hi", H)
        w_lo = signal("w_lo", H)
        y1_rdy = signal("y1_rdy", MT)
        x1_rdy = signal("x1_rdy", 1)
        q_hi = signal("q_hi", 1)
        q_lo = signal("q_lo", 1)
        q_st = [signal(f"q_st{g}", 3 * HG, 16) for g in range(MT)]
        c_ld = signal("c_ld", 1, 16)
        am_c_rdy = signal("am_c_rdy", 1)
        amr_c_rdy = signal("amr_c_rdy", 1)
        cs_step = signal("cs_step", 3)
        k_hi = signal("k_hi", 1)
        k_lo = signal("k_lo", 1)
        k_st = [signal(f"k_st{g}", 3 * HG, 16) for g in range(MT)]
        ct_ld = signal("ct_ld", 1, 16)
        xsc_rdy = signal("xsc_rdy", 1)
        s1_mm = signal("s1_mm", TILES)
        s1_max = signal("s1_max", TILES)
        nt_mm = signal("nt_mm", MT)
        nm_hi = signal("nm_hi", MT)
        nm_lo = signal("nm_lo", MT)
        nm_st = signal("nm_st", 2 * MT, 16)
        s2_mm = signal("s2_mm", TILES)
        s2_exp = signal("s2_exp", TILES)
        p_add = signal("p_add", TILES)
        pv_mm = signal("pv_mm", 8)
        den_mm = signal("den_mm", MT)
        den_inv = signal("den_inv", 2 * MT)
        o_read = signal("o_read", MT)
        x1_copy = signal("x1_copy", 1)
        y2_rdy = signal("y2_rdy", MT)
        x2_rdy = signal("x2_rdy", 1)
        x2_hi = signal("x2_hi", 1)
        x2_lo = signal("x2_lo", 1)
        xt_mm = signal("xt_mm", 2)
        xt_ev = signal("xt_ev", 2)
        u_mm = signal("u_mm", PAIRS)
        g_mm = signal("g_mm", PAIRS)
        th_rdy = signal("th_rdy", PAIRS)
        t_rdy = signal("t_rdy", PAIRS)
        p_rdy = signal("p_rdy", PAIRS)
        h_hi = signal("h_hi", PAIRS)
        h_lo = signal("h_lo", PAIRS)
        dn_mm = signal("dn_mm", PAIRS)
        y3_rdy = signal("y3_rdy", MT)
        out_rdy = signal("out_rdy", 1)
        out_st = signal("out_st", 1, 16)
        ln_st = [signal(f"ln_st{r}", MT) for r in range(3)]
        ln_ag = [signal(f"ln_ag{r}", MT) for r in range(3)]
        ln_ve = [signal(f"ln_ve{r}", 1) for r in range(3)]
        ln_rs = [signal(f"ln_rs{r}", 1) for r in range(3)]

        block = ctx.enter_context(nc.Block())

        pause, pause_x, pause_c = (sc[:, n:n + 1] for n in (18, 19, 20))

        def run_stages(eng, stage_of):
            flags = lambda i: (i < B, 1 <= i <= B, 2 <= i <= B + 1, i + 1 < B, i >= 3)
            for i in range(3):
                stage_of(i, *flags(i))
            with eng.Fori(3, B - 1) as i:
                stage_of(i, *flags(3))
            for i in range(B - 1, B + 3):
                stage_of(i, *flags(i))

        SEQ = [(wq, 0), (wk, 0), (wq, 1), (wk, 1), (wq, 2), (wk, 2), (fcT, None), (wv, 0), (wv, 1), (wv, 2)]
        SLOT = [0, 1, 2, 0, 1, 2, 0, 1, 2, 1]
        SLOT_READ = {3: KT, 4: KT, 5: 2 * KT, 6: 2 * KT, 7: 3 * KT, 8: 3 * KT, 9: 4 * KT}
        ring_of = lambda n: ring[SLOT[n]]

        @block.sync
        def _(sp):
            sp.dma_start(fcb_b[:, :], fcb.partition_broadcast(P)).then_inc(small_ld.sem, 16)
            sp.dma_start(gam[:, :], gamma.partition_broadcast(P)).then_inc(small_ld.sem, 16)

            def load_w(n):
                w, h = SEQ[n]
                src = (w[h] if h is not None else w).rearrange("(k p) e -> p k e", p=P)
                if n >= 3:
                    sp.wait_ge(ab_mm.sem, ab_mm.at(0, SLOT_READ[n]))
                sp.dma_start(ring_of(n)[:, :].rearrange("p (k e) -> p k e", k=KT), src).then_inc(
                    w_ld[SLOT[n]].sem, 16)

            def load_f(m, c):
                src = [wu, wg, wd][m].rearrange("(k p) f -> p k f", p=P)
                sp.wait_ge(quant.sem, quant.at(0, 4 * (m - 1) + c + 1)) if m else None
                if m < 2:
                    sp.dma_start(stg[:, c, :], src[:, c, :]).then_inc(f_ld[c].sem, 16)
                else:
                    sp.dma_start(stg[:, c, :].rearrange("p (k e) -> p k e", e=E),
                                 src[:, 4 * c:4 * c + 4, :]).then_inc(f_ld[c].sem, 16)

            for n in range(3):
                load_w(n)
            for c in range(4):
                load_f(0, c)
            for n in range(3, 7):
                load_w(n)
            sp.dma_start(stage[:, :].rearrange("p (k n) -> p k n", k=KT),
                         xT[0].rearrange("(k p) n -> p k n", p=P)).then_inc(xT_ld.sem, 16)
            for c in range(4):
                load_f(1, c)
            for n in range(7, 10):
                load_w(n)
            for c in range(4):
                load_f(2, c)

            def stages(i, att, cross, ffn, nxt, last_out):
                b, f = i - 1, i - 2
                if cross:
                    sp.wait_ge(consts.sem, 7)
                    sp.wait_ge(pv_mm.sem, pv_mm.at(b - 1, 8))
                    sp.dma_start(keys_t[:, :, :], ctx_t[b].rearrange("(k p) n -> p k n", p=P)).then_inc(
                        ct_ld.sem, 16)
                if att:
                    sp.wait_ge(consts.sem, 7)
                    sp.wait_ge(xT_lo.sem, xT_lo.at(i, 1))
                    sp.dma_start(stage[:, :].rearrange("p (m e) -> p m e", m=MT),
                                 ctx_n[i].rearrange("(m p) e -> p m e", p=P)).then_inc(c_ld.sem, 16)
                if last_out:
                    sp.wait_ge(consts.sem, 7)
                    sp.wait_ge(out_rdy.sem, out_rdy.at(i - 3, 1))
                    sp.dma_start(out[i - 3].rearrange("(m p) e -> p m e", p=P), x2[:, :, :]).then_inc(
                        out_st.sem, 16)
                if att:
                    sp.wait_ge(consts.sem, 7)
                    sp.wait_ge(x1_copy.sem, x1_copy.at(i - 1, 1))
                    sp.dma_start(xn[:, :, :], x[i].rearrange("(m p) e -> p m e", p=P)).then_inc(xn_ld.sem, 16)
                if nxt:
                    sp.wait_ge(consts.sem, 7)
                    sp.wait_ge(k_lo.sem, k_lo.at(i, 1))
                    sp.dma_start(stage[:, :].rearrange("p (k n) -> p k n", k=KT),
                                 xT[i + 1].rearrange("(k p) n -> p k n", p=P)).then_inc(xT_ld.sem, 16)
                if cross:
                    for grp in range(MT):
                        for s in range(2):
                            rdy = (nm_hi, nm_lo)[s]
                            sp.wait_ge(rdy.sem, rdy.at(b, grp + 1))
                            sp.dma_start(Qst[96 + s:97 + s, HG * grp:HG * (grp + 1), :].rearrange(
                                "p h (t c) -> p (h t) c", c=P), nm[:, grp, s, :]).then_inc(nm_st.sem, 16)
                if att:
                    for grp in range(MT):
                        if cross:
                            sp.wait_ge(s2_mm.sem, s2_mm.at(b, GT * (grp + 1)))
                        for src, dst, order, done, rdy in ((ksplit, Kst, (0, 0, 1), k_st[grp], k_lo),
                                                           (hl, Qst, (0, 1, 0), q_st[grp], q_lo)):
                            sp.wait_ge(rdy.sem, rdy.at(i, 1))
                            for j, s in enumerate(order):
                                for hd in range(HG):
                                    sp.dma_start(dst[32 * j:32 * j + 32, HG * grp + hd, :],
                                                 src[32 * hd:32 * hd + 32, s, grp, :]).then_inc(done.sem, 16)

            run_stages(sp, stages)
            sp.wait_ge(consts.sem, 7)
            sp.wait_ge(out_st.sem, out_st.at(B - 1, 1))

        @block.gpsimd
        def _(pool):
            g = nc.gpsimd
            g.memset(ones[:, :], 1.0).then_inc(consts.sem, 1)
            g.memset(mhalf[:, :], -0.5).then_inc(consts.sem, 1)
            g.memset(eps[:, :], EPS_LN).then_inc(consts.sem, 1)
            g.memset(id16[:, :], 0.0).then_inc(consts.sem, 1)
            g.memset(id32[:, :], 0.0).then_inc(consts.sem, 1)
            pool.wait_ge(consts.sem, consts.at(0, 5))
            for t in (id16, id32):
                g.affine_select(out=t[:, :], in_=t[:, :], compare_op=ALU.not_equal, fill=1.0, base=0,
                                pattern=[[-1, P]], channel_multiplier=1).then_inc(consts.sem, 1)

            def all_max(rdy, done, dst, src, b, k=1):
                pool.wait_ge(rdy.sem, rdy.at(b, k))
                if not isinstance(b, int):
                    g.tensor_tensor(pause_c if rdy is am_c_rdy else pause_x, mhalf[:, 0:1], mhalf[:, 0:1],
                                    ALU.add)
                g.partition_all_reduce(dst, src, P, RMAX).then_inc(done.sem, 1)

            def rstd_of(r, b):
                pool.wait_ge(ln_ag[r].sem, ln_ag[r].at(b, MT))
                g.tensor_tensor(ve[r][:, :], mv[r][:, :, 1], eps[:, :], ALU.add).then_inc(ln_ve[r].sem, 1)
                pool.wait_ge(ln_ve[r].sem, ln_ve[r].at(b, 1))
                g.tensor_tensor(rstd[r][:, :], ve[r][:, :], mhalf[:, :], ALU.pow).then_inc(ln_rs[r].sem, 1)

            all_max(am_w_rdy, amr_w_rdy, amr_w, am_w, 0, 1)
            all_max(am_x_rdy, amr_x_rdy, amr_x, am_x, 0)
            all_max(am_w_rdy, amr_w_rdy, amr_w, am_w, 0, 2)
            pool.wait_ge(small_ld.sem, small_ld.at(0, 2))

            def stages(i, att, cross, ffn, nxt, last_out):
                b, f = i - 1, i - 2

                def add_tiles(u):
                    lt, grp = u % KT, u // KT
                    for v in range(HG):
                        n = u * HG + v
                        pool.wait_ge(s2_exp.sem, s2_exp.at(b, n + 1))
                        if lt == 0:
                            if v == 0:
                                pool.wait_ge(den_mm.sem, den_mm.at(b, grp))
                            g.tensor_tensor(Psum[:, v, :], Pe[:, v, :], ones[:, 0:1].to_broadcast([P, E]),
                                            ALU.mult).then_inc(p_add.sem, 1)
                        else:
                            pool.wait_ge(p_add.sem, p_add.at(b, n - HG + 1))
                            g.tensor_tensor(Psum[:, v, :], Psum[:, v, :], Pe[:, v, :],
                                            ALU.add).then_inc(p_add.sem, 1)

                if last_out:
                    rstd_of(2, i - 3)
                if ffn:
                    rstd_of(1, f)
                if att:
                    all_max(am_c_rdy, amr_c_rdy, amr_c, am_c, i)
                    pool.wait_ge(xn_ld.sem, xn_ld.at(i, 1))
                    g.tensor_tensor(xn[:, :, :], xn[:, :, :],
                                    fcb_b[:, :].rearrange("p (a e) -> p a e", a=1).to_broadcast([P, MT, E]),
                                    ALU.add).then_inc(xb_rdy.sem, 1)
                for u in range(8):
                    if u == 2 and att:
                        rstd_of(0, i)
                    if u == 5 and nxt:
                        all_max(am_x_rdy, amr_x_rdy, amr_x, am_x, i + 1)
                    if cross:
                        add_tiles(u)

            run_stages(pool, stages)

        @block.scalar
        def _(act):
            a = nc.scalar

            def tiles_ab(first):
                for t in range(first, first + H * KT):
                    act.wait_ge(ab_mm.sem, ab_mm.at(0, t + 1))
                    if t == H * KT:
                        act.wait_ge(ab_lo.sem, ab_lo.at(0, 1))
                    a.activation(hold[:, (t - first) // KT, (t - first) % KT, :], L[t % 2][:, :],
                                 ACT.Copy).then_inc(ab_ev.sem, 1)

            def split_hi(dst, n):
                act.wait_ge(sw_rdy.sem, sw_rdy.at(0, n + 1))
                a.activation(dst[:, 0].rearrange("p h k e -> p (h k e)"), work_b[:, :], ACT.Copy,
                             scale=s_w).then_inc(ab_hi.sem, 1)

            def xT_split_hi(b):
                act.wait_ge(xs_step.sem, xs_step.at(b, 5))
                a.activation(xTs[:, 0].rearrange("p k n -> p (k n)"), stage[:, :], ACT.Copy,
                             scale=s_x).then_inc(xT_hi.sem, 1)

            tiles_ab(0)
            split_hi(A, 0)
            tiles_ab(H * KT)
            split_hi(Bm, 1)
            xT_split_hi(0)

            def stages(i, att, cross, ffn, nxt, last_out):
                b, f = i - 1, i - 2

                def weight_hi(h):
                    act.wait_ge(wsc_rdy.sem, wsc_rdy.at(i, h + 1))
                    for m in range(MT):
                        last = a.activation(ws[:, 0, h, m, :], we[:, h % 2, m, :], ACT.Copy,
                                            scale=r4[:, h, m:m + 1])
                    last.then_inc(w_hi.sem, 1)

                for j, (kind, h, m) in enumerate(BLOCKS):
                    if att:
                        act.wait_ge(l_mm.sem, l_mm.at(i, j + 1))
                        if kind == "S":
                            act.wait_ge(bias_rdy.sem, bias_rdy.at(i, h + 1))
                            if h == 2:
                                act.wait_ge(w_lo.sem, w_lo.at(i, 1))
                            for mt in range(MT):
                                last = a.activation(we[:, h % 2, mt, :], L[j % 2][:, mt * N:mt * N + N], ACT.Exp,
                                                    bias=nb[:, h, mt:mt + 1], scale=esc,
                                                    accum_out=sm[:, h, mt:mt + 1])
                            last.then_inc(e_done.sem, 1)
                        else:
                            dst = (Gs[:, h % 2, 0, 2 * m:2 * m + 2, :].rearrange("p k n -> p (k n)")
                                   if kind == "G" else Vs[:, 0, h, m, :])
                            a.activation(dst, L[j % 2][:, :], ACT.Copy, scale=DOWN).then_inc(gv_hi.sem, 1)
                        if j - 1 in SB:
                            weight_hi(SB.index(j - 1))
                    if ffn and j == 10:
                        act.wait_ge(x2_rdy.sem, x2_rdy.at(f, 1))
                        if cross:
                            for grp in range(MT):
                                act.wait_ge(q_st[grp].sem, q_st[grp].at(b, 3 * HG))
                        a.activation(hl[:, 0].rearrange("p m e -> p (m e)"),
                                     x2[:, :, :].rearrange("p m e -> p (m e)"), ACT.Copy,
                                     scale=X2S).then_inc(x2_hi.sem, 1)
                    if cross and j == 10:
                        act.wait_ge(q_lo.sem, q_lo.at(b, 1))
                        a.activation(x1[:, :, :].rearrange("p m e -> p (m e)"),
                                     xn[:, :, :].rearrange("p m e -> p (m e)"), ACT.Copy).then_inc(x1_copy.sem, 1)
                    if att and j == 11:
                        act.wait_ge(cs_step.sem, cs_step.at(i, 3))
                        for grp in range(MT):
                            act.wait_ge(k_st[grp].sem, k_st[grp].at(i - 1, 3 * HG))
                        a.activation(ksplit[:, 0].rearrange("p m e -> p (m e)"), stage[:, :], ACT.Copy,
                                     scale=s_c).then_inc(k_hi.sem, 1)
                    if ffn and j in (11, 13):
                        s = (j - 11) // 2
                        act.wait_ge(xt_mm.sem, xt_mm.at(f, s + 1))
                        a.activation(x2T[:, s].rearrange("p k n -> p (k n)"), T16, ACT.Copy).then_inc(
                            xt_ev.sem, 1)

                def exps(u, v):
                    n = u * HG + v
                    act.wait_ge(s2_mm.sem, s2_mm.at(b, n + 1))
                    if n >= HG:
                        act.wait_ge(p_add.sem, p_add.at(b, n - HG + 1))
                    a.activation(Pe[:, v, :], S[0][:, :], ACT.Exp, scale=xsc).then_inc(s2_exp.sem, 1)

                def hidden_hi(u):
                    act.wait_ge(p_rdy.sem, p_rdy.at(f, u + 1))
                    a.activation(hs[:, u % 2, 0].rearrange("p e n -> p (e n)"), th[:, u % 2, :],
                                 ACT.Copy).then_inc(h_hi.sem, 1)

                for u in range(8):
                    if cross:
                        if u == 0:
                            act.wait_ge(xsc_rdy.sem, xsc_rdy.at(b, 1))
                        exps(u, 0)
                    if ffn and u:
                        hidden_hi(u - 1)
                    if cross:
                        exps(u, 1)
                    if ffn:
                        act.wait_ge(u_mm.sem, u_mm.at(f, u + 1))
                        a.activation(th[:, u % 2, :], bank["U"][:, :], ACT.Tanh, scale=half_u).then_inc(
                            th_rdy.sem, 1)
                    if cross:
                        exps(u, 2)
                        exps(u, 3)
                    if u == 2 and att:
                        act.wait_ge(x1_rdy.sem, x1_rdy.at(i, 1))
                        if ffn:
                            act.wait_ge(xt_mm.sem, xt_mm.at(f, 2))
                        a.activation(hl[:, 0].rearrange("p m e -> p (m e)"),
                                     xn[:, :, :].rearrange("p m e -> p (m e)"), ACT.Copy,
                                     scale=QS).then_inc(q_hi.sem, 1)
                    if u == 6 and nxt:
                        xT_split_hi(i + 1)
                if ffn:
                    hidden_hi(PAIRS - 1)

            run_stages(act, stages)

        @block.tensor
        def _(pe):
            t_ = nc.tensor
            pe.wait_ge(consts.sem, consts.at(0, 7))
            for t in range(2 * H * KT):
                h, et = t // KT % H, t % KT
                if t < H * KT:
                    nl, nr = 2 * h, 2 * h + 1
                else:
                    nl, nr = 7 + h, 6
                if et == 0:
                    for n in (nl, nr):
                        pe.wait_ge(w_ld[SLOT[n]].sem, w_ld[SLOT[n]].at(0, SLOT[:n + 1].count(SLOT[n])))
                if t >= 2:
                    pe.wait_ge(ab_ev.sem, ab_ev.at(0, t - 1))
                lhs = ring_of(nl).rearrange("p (k e) -> p k e", k=KT)
                rhs = ring_of(nr).rearrange("p (k e) -> p k e", k=KT)
                for k in range(KT):
                    last = t_.matmul(L[t % 2][:, :], lhs[:, k, et * P:(et + 1) * P], rhs[:, k, :],
                                     start=(k == 0), stop=(k == KT - 1))
                last.then_inc(ab_mm.sem, 1)
                if t in (H * KT - 1, H * KT + 5, 2 * H * KT - 1):
                    m = (H * KT - 1, H * KT + 5, 2 * H * KT - 1).index(t)
                    pe.wait_ge(f_tot.sem, f_tot.at(0, m + 1))
                    t_.matmul(bank["U"][:, m:m + 1], ones[:, :], tot[:, m:m + 1], start=True,
                              stop=True).then_inc(f_mm.sem, 1)

            def split_products(dst, terms, between=None):
                for n, (lhs, rhs) in enumerate(terms):
                    if between and n == len(terms) // 2:
                        between()
                    last = t_.matmul(dst, lhs, rhs, start=(n == 0), stop=(n == len(terms) - 1))
                return last

            PARTS = ((0, 0), (0, 1), (1, 0))

            def stages(i, att, cross, ffn, nxt, last_out):
                b, f = i - 1, i - 2

                def s1(t):
                    h, qt = t // KT, t % KT
                    if t % GT == 0:
                        grp = t // GT
                        pe.wait_ge(q_st[grp].sem, q_st[grp].at(b, 3 * HG))
                        pe.wait_ge(k_st[grp].sem, k_st[grp].at(b, 3 * HG))
                    if t:
                        pe.wait_ge(s1_max.sem, s1_max.at(b, t))
                    t_.matmul(S[1][:, :], Qst[0:96, h, qt * P:(qt + 1) * P], Kst[0:96, h, :], start=True,
                              stop=True).then_inc(s1_mm.sem, 1)

                def max_rows(grp):
                    pe.wait_ge(s1_max.sem, s1_max.at(b, GT * (grp + 1)))
                    if ffn:
                        pe.wait_ge(xt_ev.sem, xt_ev.at(f, grp + 1))
                    t_.transpose(bank["T"][0:GT, 0:P], xmx[:, GT * grp:GT * (grp + 1)],
                                 id32[:, :]).then_inc(nt_mm.sem, 1)

                def denom(batch, grp):
                    pe.wait_ge(p_add.sem, p_add.at(batch, (grp + 1) * GT))
                    pe.wait_ge(nm_lo.sem, nm_lo.at(batch, MT))
                    for v in range(HG):
                        last = t_.matmul(bank["T"][v * DH:(v + 1) * DH, :], ones[:, 0:DH], Psum[:, v, :],
                                         start=True, stop=True, skip_group_check=True)
                    last.then_inc(den_mm.sem, 1)

                for j, (kind, h, m) in enumerate(BLOCKS):
                    pend = list(s1_of.get(j, ())) if cross else []

                    def s1_next():
                        if pend:
                            s1(pend.pop(0))

                    if att:
                        bk = L[j % 2]
                        if j == 0:
                            pe.wait_ge(xT_lo.sem, xT_lo.at(i, 1))
                            if isinstance(i, int) and i == 0:
                                pe.wait_ge(ab_lo.sem, ab_lo.at(0, 2))
                        if j < 2:
                            if ffn:
                                pe.wait_ge(y3_rdy.sem, y3_rdy.at(f - 1, MT))
                            pe.wait_ge(y1_rdy.sem, y1_rdy.at(i - 1, MT))
                        elif (j - 2) in SB:
                            pe.wait_ge(e_done.sem, e_done.at(i, SB.index(j - 2) + 1))
                        else:
                            pe.wait_ge(gv_lo.sem, gv_lo.at(i, GV.index(j - 2) + 1))
                        if kind == "G":
                            for c in range(2):
                                cols = slice((2 * m + c) * P, (2 * m + c + 1) * P)
                                last = split_products(bk[:, c * N:(c + 1) * N], [
                                    (A[:, pl, h, k, cols], xTs[:, pr, k, :]) for pl, pr in PARTS for k in range(KT)])
                                if c == 0:
                                    s1_next()
                        elif kind == "S":
                            pe.wait_ge(gv_lo.sem, gv_lo.at(i, GV.index(BLOCKS.index(("G", h, 1))) + 1))
                            for c in range(MT):
                                last = split_products(bk[:, c * N:(c + 1) * N], [
                                    (xTs[:, pl, k, c * P:(c + 1) * P], Gs[:, h % 2, pr, k, :])
                                    for pl, pr in PARTS for k in range(KT)])
                                if c == 0:
                                    s1_next()
                        else:
                            last = split_products(bk[:, :], [
                                (xTs[:, pl, k, m * P:(m + 1) * P], Bm[:, pr, h, k, :])
                                for pl, pr in PARTS for k in range(KT)], s1_next)
                        last.then_inc(l_mm.sem, 1)
                    while pend:
                        s1_next()
                    if ffn and j == 0:
                        denom(f, 1)
                    if cross and j == S1_TURN:
                        max_rows(0)
                    if ffn and j in (11, 13):
                        s = (j - 11) // 2
                        rdy = (x2_hi, x2_lo)[s]
                        pe.wait_ge(rdy.sem, rdy.at(f, 1))
                        if s == 0:
                            pe.wait_ge(den_inv.sem, den_inv.at(f, 2 * MT))
                        else:
                            pe.wait_ge(xt_ev.sem, xt_ev.at(f, 1))
                            if cross:
                                pe.wait_ge(nm_lo.sem, nm_lo.at(b, 1))
                        for k in range(KT):
                            for mt in range(MT):
                                c0 = k * N + mt * P
                                last = t_.transpose(T16[:, c0:c0 + P], hl[:, s, mt, k * P:(k + 1) * P], id16[:, :])
                        last.then_inc(xt_mm.sem, 1)
                if att:
                    pe.wait_ge(w_lo.sem, w_lo.at(i, H))
                    pe.wait_ge(gv_lo.sem, gv_lo.at(i, NGV - 1))
                    for n in range(MT):
                        j = NBLK + n
                        for h in range(H):
                            for m in range(MT):
                                if (h, m) == (H - 1, MT - 1):
                                    pe.wait_ge(gv_lo.sem, gv_lo.at(i, NGV))
                                for pl, pr in PARTS:
                                    last = t_.matmul(L[j % 2][:, :], ws[:, pl, h, m, n * P:(n + 1) * P],
                                                     Vs[:, pr, h, m, :], start=(h == m == pl == pr == 0),
                                                     stop=(h == H - 1 and m == MT - 1 and pl == 1))
                        last.then_inc(l_mm.sem, 1)

                def s2(u, v):
                    n = u * HG + v
                    h, lt = HG * (u // KT) + v, u % KT
                    if n % GT == 0:
                        pe.wait_ge(nm_st.sem, nm_st.at(b, 2 * (n // GT + 1)))
                        pe.wait_ge(krow.sem, krow.at(0, 1))
                    if n:
                        pe.wait_ge(s2_exp.sem, s2_exp.at(b, n))
                    t_.matmul(S[0][:, :], Kst[0:98, h, lt * P:(lt + 1) * P], Qst[0:98, h, :], start=True,
                              stop=True).then_inc(s2_mm.sem, 1)

                def hidden(u, W, dst, done, free):
                    for e in range(2):
                        v = 2 * (dst is bank["G"]) + e
                        if ffn:
                            if e == 0:
                                pe.wait_ge(free.sem, free.at(f, u))
                            cols = slice((2 * u + e) * P, (2 * u + e + 1) * P)
                        for s in range(2):
                            if ffn:
                                for k in range(KT):
                                    last = t_.matmul(dst[:, e * N:(e + 1) * N], W[:, k, cols], x2T[:, s, k, :],
                                                     start=(s == 0 and k == 0), stop=(s == 1 and k == KT - 1))
                                if e == 1 and s == 1:
                                    last.then_inc(done.sem, 1)
                            if cross and s == 1:
                                s2(u, v)
                            if cross and s == 0 and u < S1_SLOTS:
                                s1(S1_BLOCKS + HG * u + v)

                def down(u):
                    pe.wait_ge(h_lo.sem, h_lo.at(f, u + 1))
                    if u == 0:
                        if att:
                            pe.wait_ge(y1_rdy.sem, y1_rdy.at(i, MT))
                        pe.wait_ge(y3_rdy.sem, y3_rdy.at(f - 1, MT))
                    for n in range(MT):
                        for e in range(2):
                            for s in range(2):
                                last = t_.matmul(L[n][:, :], hs[:, u % 2, s, e, n * P:(n + 1) * P],
                                                 Wd[:, 2 * u + e, :], start=(u == 0 and e == 0 and s == 0),
                                                 stop=(u == PAIRS - 1 and e == 1 and s == 1))
                    last.then_inc(dn_mm.sem, 1)

                def pv(u):
                    grp, lt = u // KT, u % KT
                    if u == 0:
                        pe.wait_ge(ct_ld.sem, ct_ld.at(b, 1))
                    if lt == 0:
                        pe.wait_ge(o_read.sem, o_read.at(b, grp))
                    pe.wait_ge(s2_exp.sem, s2_exp.at(b, HG * (u + 1)))
                    for v in range(HG):
                        c0 = grp * P + v * DH
                        last = t_.matmul(bank["O"][v * DH:(v + 1) * DH, :], keys_t[:, lt, c0:c0 + DH], Pe[:, v, :],
                                         start=(lt == 0), stop=(lt == KT - 1), skip_group_check=True)
                    last.then_inc(pv_mm.sem, 1)

                if ffn:
                    pe.wait_ge(xt_ev.sem, xt_ev.at(f, 2))
                for u in range(8):
                    hidden(u, Wu, bank["U"], u_mm, t_rdy)
                    if u == KT and cross:
                        denom(b, 0)
                    hidden(u, Wg, bank["G"], g_mm, p_rdy)
                    if ffn and u:
                        down(u - 1)
                    if cross:
                        if u == S1_SLOTS - 1:
                            max_rows(1)
                        pv(u)
                if ffn:
                    down(PAIRS - 1)

            run_stages(pe, stages)

        @block.vector
        def _(dve):
            v_ = nc.vector
            steps = [0]

            def step(ins):
                steps[0] += 1
                ins.then_inc(prep.sem, 1)
                dve.wait_ge(prep.sem, prep.at(0, steps[0]))

            def x_absmax(b):
                dve.wait_ge(xT_ld.sem, xT_ld.at(b, 1))
                v_.tensor_reduce(am_x, stage[:, :], AXX, ALU.max, apply_absolute_value=True).then_inc(
                    am_x_rdy.sem, 1)

            def x_scales(b):
                dve.wait_ge(amr_x_rdy.sem, amr_x_rdy.at(b, 1))
                v_.tensor_scalar(amr_x, amr_x, 1e-30, None, ALU.max).then_inc(xs_step.sem, 1)
                dve.wait_ge(xs_step.sem, xs_step.at(b, 1))
                v_.reciprocal(inv_x, amr_x).then_inc(xs_step.sem, 1)
                v_.scalar_tensor_tensor(esc, amr_x, amr_x, c_esc, ALU.mult, ALU.mult).then_inc(xs_step.sem, 1)
                v_.tensor_tensor(asc, amr_x, c_asc, ALU.mult).then_inc(xs_step.sem, 1)
                dve.wait_ge(xs_step.sem, xs_step.at(b, 2))
                v_.tensor_scalar(s_x, inv_x, TOP, None, ALU.mult).then_inc(xs_step.sem, 1)

            def x_lo(b):
                dve.wait_ge(xT_hi.sem, xT_hi.at(b, 1))
                v_.scalar_tensor_tensor(xTs[:, 1].rearrange("p k n -> p (k n)"), stage[:, :], s_x,
                                        xTs[:, 0].rearrange("p k n -> p (k n)"), ALU.mult,
                                        ALU.subtract).then_inc(xT_lo.sem, 1)

            def matrix_scale(n, back, const):
                dve.wait_ge(ab_ev.sem, ab_ev.at(0, (n + 1) * H * KT))
                v_.tensor_reduce(am_w, work_b[:, :], AXX, ALU.max, apply_absolute_value=True).then_inc(
                    am_w_rdy.sem, 1)
                dve.wait_ge(amr_w_rdy.sem, amr_w_rdy.at(0, n + 1))
                step(v_.tensor_scalar(amr_w, amr_w, 1e-30, None, ALU.max))
                step(v_.reciprocal(inv_w, amr_w))
                step(v_.tensor_scalar(back, amr_w, const, None, ALU.mult))
                v_.tensor_scalar(s_w, inv_w, TOP, None, ALU.mult).then_inc(sw_rdy.sem, 1)

            def matrix_lo(dst, n):
                dve.wait_ge(ab_hi.sem, ab_hi.at(0, n + 1))
                v_.scalar_tensor_tensor(dst[:, 1].rearrange("p h k e -> p (h k e)"), work_b[:, :], s_w,
                                        dst[:, 0].rearrange("p h k e -> p (h k e)"), ALU.mult,
                                        ALU.subtract).then_inc(ab_lo.sem, 1)

            def ternary(m):
                for c in range(4):
                    dve.wait_ge(f_ld[c].sem, f_ld[c].at(0, m + 1))
                    last = v_.tensor_reduce(part[:, m, 4 * c:4 * c + 4],
                                            stg[:, c, :].rearrange("p (q e) -> p q e", e=E), AXX, ALU.add,
                                            apply_absolute_value=True)
                step(last)
                v_.tensor_reduce(tot[:, m:m + 1], part[:, m, :], AXX, ALU.add).then_inc(f_tot.sem, 1)
                dve.wait_ge(f_mm.sem, f_mm.at(0, m + 1))
                step(v_.tensor_scalar(mean_w[:, m:m + 1], bank["U"][:, m:m + 1], 1.0 / (E * F), EPS_Q, ALU.mult,
                                      ALU.add))
                step(v_.tensor_scalar(thr[:, m:m + 1], mean_w[:, m:m + 1], 0.5, None, ALU.mult))
                step(v_.tensor_scalar(nthr[:, m:m + 1], mean_w[:, m:m + 1], -0.5, None, ALU.mult))
                W = [Wu, Wg, Wd][m]
                for c in range(4):
                    dst = W[:, c, :] if m < 2 else W[:, 4 * c:4 * c + 4, :].rearrange("p k e -> p (k e)")
                    step(v_.tensor_scalar(dst, stg[:, c, :], nthr[:, m:m + 1], None, ALU.is_lt))
                    v_.scalar_tensor_tensor(dst, stg[:, c, :], thr[:, m:m + 1], dst, ALU.is_gt,
                                            ALU.subtract).then_inc(quant.sem, 1)

            def ln_stats(r, b, src, m):
                v_.bn_stats(bst[r][:, m, :], src[:, m, :]).then_inc(ln_st[r].sem, 1)
                if m == MT - 1:
                    dve.wait_ge(ln_st[r].sem, ln_st[r].at(b, MT))
                    v_.memset(pause, 0.0)
                    for n in range(MT):
                        v_.bn_aggr(mv[r][:, n, :], bst[r][:, n, :]).then_inc(ln_ag[r].sem, 1)

            def ln_apply(r, b, dst, src):
                dve.wait_ge(ln_rs[r].sem, ln_rs[r].at(b, 1))
                for m in range(MT):
                    last = v_.tensor_scalar(dst[:, m, :], src[:, m, :], mv[r][:, m, 0:1], rstd[r][:, m:m + 1],
                                            ALU.subtract, ALU.mult)
                return last

            ternary(0)
            matrix_scale(0, c_esc, ESC)
            x_absmax(0)
            matrix_lo(A, 0)
            ternary(1)
            matrix_scale(1, c_asc, ASC)
            matrix_lo(Bm, 1)
            x_scales(0)
            x_lo(0)
            ternary(2)
            v_.memset(Kst[96:98, :, :], MROW).then_inc(krow.sem, 1)
            step(v_.tensor_scalar(half_u, mean_w[:, 0:1], 0.5 / X2S, None, ALU.mult))
            step(v_.tensor_tensor(gd, mean_w[:, 1:2], mean_w[:, 2:3], ALU.mult))
            step(v_.tensor_scalar(gd, gd, mean_w[:, 0:1], DSC, ALU.mult, ALU.mult))
            dve.wait_ge(small_ld.sem, small_ld.at(0, 2))

            def stages(i, att, cross, ffn, nxt, last_out):
                b, f = i - 1, i - 2

                def weight_scale(h):
                    dve.wait_ge(e_done.sem, e_done.at(i, h + 1))
                    v_.reciprocal(rs[:, h, :], sm[:, h, :]).then_inc(sum_inv.sem, 1)
                    dve.wait_ge(sum_inv.sem, sum_inv.at(i, h + 1))
                    v_.tensor_scalar(r4[:, h, :], rs[:, h, :], WTOP, None, ALU.mult).then_inc(wsc_rdy.sem, 1)

                def weight_lo(h):
                    dve.wait_ge(w_hi.sem, w_hi.at(i, h + 1))
                    for m in range(MT):
                        last = v_.scalar_tensor_tensor(ws[:, 1, h, m, :], we[:, h % 2, m, :], r4[:, h, m:m + 1],
                                                       ws[:, 0, h, m, :], ALU.mult, ALU.subtract)
                    last.then_inc(w_lo.sem, 1)

                def cross_max(t):
                    dve.wait_ge(s1_mm.sem, s1_mm.at(b, t + 1))
                    v_.tensor_reduce(xmx[:, t:t + 1], S[1][:, :], AXX, ALU.max).then_inc(s1_max.sem, 1)

                def neg_max(grp):
                    dve.wait_ge(nt_mm.sem, nt_mm.at(b, grp + 1))
                    dve.wait_ge(nm_st.sem, nm_st.at(b - 1, 2 * MT))
                    v_.tensor_scalar(nm[:, grp, 0, :], bank["T"][0:GT, 0:P], -1.0 / MROW, None,
                                     ALU.mult).then_inc(nm_hi.sem, 1)
                    dve.wait_ge(nm_hi.sem, nm_hi.at(b, grp + 1))
                    v_.scalar_tensor_tensor(nm[:, grp, 1, :], bank["T"][0:GT, 0:P], -1.0 / MROW,
                                            nm[:, grp, 0, :], ALU.mult, ALU.subtract).then_inc(nm_lo.sem, 1)

                def cross_inv(batch, grp, half):
                    cols = slice(half * E // 2, (half + 1) * E // 2)
                    dve.wait_ge(den_mm.sem, den_mm.at(batch, grp + 1))
                    v_.reciprocal(den[:, cols], bank["T"][:, cols]).then_inc(den_inv.sem, 1)

                def cross_out(batch, grp):
                    dve.wait_ge(den_inv.sem, den_inv.at(batch, 2 * (grp + 1)))
                    dve.wait_ge(pv_mm.sem, pv_mm.at(batch, KT * (grp + 1)))
                    v_.tensor_tensor(den, bank["O"][:, :], den, ALU.mult).then_inc(o_read.sem, 1)
                    dve.wait_ge(o_read.sem, o_read.at(batch, grp + 1))
                    if grp == 0:
                        dve.wait_ge(x1_copy.sem, x1_copy.at(batch, 1))
                    v_.scalar_tensor_tensor(x1[:, grp, :], den, gam[:, 0:1], x1[:, grp, :], ALU.mult,
                                            ALU.add).then_inc(y2_rdy.sem, 1)

                for j, (kind, h, m) in enumerate(BLOCKS):
                    if cross:
                        for t in s1_of[j][:1]:
                            cross_max(t)
                    if att:
                        bk = L[j % 2]
                        if kind == "S":
                            dve.wait_ge(l_mm.sem, l_mm.at(i, j + 1))
                            v_.tensor_reduce(cm[:, h, :], bk[:, :].rearrange("p (m n) -> p m n", m=MT), AXX,
                                             ALU.max).then_inc(cmax.sem, 1)
                            dve.wait_ge(cmax.sem, cmax.at(i, h + 1))
                            v_.tensor_scalar(nb[:, h, :], cm[:, h, :], esc, -1.0, ALU.mult,
                                             ALU.mult).then_inc(bias_rdy.sem, 1)
                        else:
                            dve.wait_ge(gv_hi.sem, gv_hi.at(i, GV.index(j) + 1))
                            hi, lo = ([Gs[:, h % 2, s, 2 * m:2 * m + 2, :].rearrange("p k n -> p (k n)")
                                       for s in range(2)] if kind == "G" else [Vs[:, s, h, m, :] for s in range(2)])
                            v_.scalar_tensor_tensor(lo, bk[:, :], DOWN, hi, ALU.mult,
                                                    ALU.subtract).then_inc(gv_lo.sem, 1)
                        if j - 1 in SB:
                            weight_scale(SB.index(j - 1))
                        if j - 2 in SB:
                            weight_lo(SB.index(j - 2))
                    if cross:
                        for t in s1_of[j][1:]:
                            cross_max(t)
                    if ffn and j in (1, 2):
                        cross_inv(f, 1, j - 1)
                    if ffn and j == 3:
                        cross_out(f, 1)
                    if last_out and j in (0, 5):
                        ln_stats(2, i - 3, x2, j // 5)
                    if last_out and j == 7:
                        ln_apply(2, i - 3, x2, x2).then_inc(out_rdy.sem, 1)
                    if ffn and j in (6, 7):
                        dve.wait_ge(y2_rdy.sem, y2_rdy.at(f, MT))
                        ln_stats(1, f, x1, j - 6)
                    if cross and j == 6:
                        dve.wait_ge(s2_exp.sem, s2_exp.at(b - 1, TILES))
                        v_.tensor_scalar(xsc, amr_c, XSC, None, ALU.mult).then_inc(xsc_rdy.sem, 1)
                    if att and j == 8:
                        dve.wait_ge(c_ld.sem, c_ld.at(i, 1))
                        v_.tensor_reduce(am_c, stage[:, :], AXX, ALU.max, apply_absolute_value=True).then_inc(
                            am_c_rdy.sem, 1)
                    if ffn and j == 10:
                        dve.wait_ge(out_st.sem, out_st.at(f - 1, 1))
                        ln_apply(1, f, x2, x1).then_inc(x2_rdy.sem, 1)
                    if att and j == 10:
                        dve.wait_ge(amr_c_rdy.sem, amr_c_rdy.at(i, 1))
                        v_.tensor_scalar(amr_c, amr_c, 1e-30, None, ALU.max).then_inc(cs_step.sem, 1)
                        dve.wait_ge(cs_step.sem, cs_step.at(i, 1))
                        v_.reciprocal(inv_c, amr_c).then_inc(cs_step.sem, 1)
                        dve.wait_ge(cs_step.sem, cs_step.at(i, 2))
                        v_.tensor_scalar(s_c, inv_c, KTOP, None, ALU.mult).then_inc(cs_step.sem, 1)
                    if ffn and j == 11:
                        dve.wait_ge(x2_hi.sem, x2_hi.at(f, 1))
                        v_.scalar_tensor_tensor(hl[:, 1], x2[:, :, :], X2S, hl[:, 0], ALU.mult,
                                                ALU.subtract).then_inc(x2_lo.sem, 1)
                    if cross and j == S1_TURN:
                        neg_max(0)
                    if att and j == 13:
                        dve.wait_ge(k_hi.sem, k_hi.at(i, 1))
                        v_.scalar_tensor_tensor(ksplit[:, 1].rearrange("p m e -> p (m e)"), stage[:, :], s_c,
                                                ksplit[:, 0].rearrange("p m e -> p (m e)"), ALU.mult,
                                                ALU.subtract).then_inc(k_lo.sem, 1)
                if att:
                    dve.wait_ge(xb_rdy.sem, xb_rdy.at(i, 1))
                    for n in range(MT):
                        dve.wait_ge(l_mm.sem, l_mm.at(i, NBLK + n + 1))
                        v_.scalar_tensor_tensor(xn[:, n, :], L[(NBLK + n) % 2][:, :], asc, xn[:, n, :], ALU.mult,
                                                ALU.add).then_inc(y1_rdy.sem, 1)

                def pair_t(u):
                    dve.wait_ge(th_rdy.sem, th_rdy.at(f, u + 1))
                    v_.scalar_tensor_tensor(th[:, u % 2, :], th[:, u % 2, :], 1.0, bank["U"][:, :], ALU.add,
                                            ALU.mult).then_inc(t_rdy.sem, 1)

                def pair_lo(u):
                    dve.wait_ge(h_hi.sem, h_hi.at(f, u + 1))
                    v_.tensor_tensor(hs[:, u % 2, 1].rearrange("p e n -> p (e n)"), th[:, u % 2, :],
                                     hs[:, u % 2, 0].rearrange("p e n -> p (e n)"),
                                     ALU.subtract).then_inc(h_lo.sem, 1)

                def pair_p(u):
                    dve.wait_ge(g_mm.sem, g_mm.at(f, u + 1))
                    dve.wait_ge(t_rdy.sem, t_rdy.at(f, u + 1))
                    v_.scalar_tensor_tensor(th[:, u % 2, :], th[:, u % 2, :], HS / 2, bank["G"][:, :], ALU.mult,
                                            ALU.mult).then_inc(p_rdy.sem, 1)

                for u in range(8):
                    def maxes(*tiles):
                        if cross and u < S1_SLOTS:
                            for v in tiles:
                                cross_max(S1_BLOCKS + HG * u + v)

                    maxes(0, 1, 2)
                    if ffn and u:
                        pair_lo(u - 1)
                    if ffn:
                        pair_t(u)
                    if u == KT and cross:
                        cross_inv(b, 0, 0)
                        cross_inv(b, 0, 1)
                        cross_out(b, 0)
                    maxes(3)
                    if ffn:
                        pair_p(u)
                    if u < MT and att:
                        dve.wait_ge(y1_rdy.sem, y1_rdy.at(i, MT))
                        ln_stats(0, i, xn, u)
                    if u == 2 and att:
                        ln_apply(0, i, xn, xn).then_inc(x1_rdy.sem, 1)
                    if u == S1_SLOTS - 1 and cross:
                        neg_max(1)
                    if u == 3 and att:
                        dve.wait_ge(q_hi.sem, q_hi.at(i, 1))
                        v_.scalar_tensor_tensor(hl[:, 1], xn[:, :, :], QS, hl[:, 0], ALU.mult,
                                                ALU.subtract).then_inc(q_lo.sem, 1)
                    if u == 4 and nxt:
                        x_absmax(i + 1)
                    if u == 5 and nxt:
                        x_scales(i + 1)
                    if u == 6 and nxt:
                        x_lo(i + 1)
                if ffn:
                    pair_lo(PAIRS - 1)
                    dve.wait_ge(dn_mm.sem, dn_mm.at(f, PAIRS))
                    for n in range(MT):
                        v_.scalar_tensor_tensor(x2[:, n, :], L[n][:, :], gd, x2[:, n, :], ALU.mult,
                                                ALU.add).then_inc(y3_rdy.sem, 1)
                    dve.wait_ge(y3_rdy.sem, y3_rdy.at(f, MT))

            run_stages(dve, stages)


def kernel(x, ctx_2048, L0_attn_Wq, L0_attn_Wk, L0_attn_Wv, L0_attn_fc_w, L0_attn_fc_b, L0_xattn_gamma,
           L0_ffn_W_up, L0_ffn_W_gate, L0_ffn_W_down):
    import numpy as np
    import concourse.bacc as bacc
    from concourse.bass_utils import run_bass_kernel_spmd

    c = np.ascontiguousarray
    arrays = {
        "x": c(x), "xT": c(np.transpose(x, (0, 2, 1))),
        "ctx_n": c(ctx_2048), "ctx_t": c(np.transpose(ctx_2048, (0, 2, 1))),
        "wq": c(L0_attn_Wq), "wk": c(L0_attn_Wk), "wv": c(L0_attn_Wv),
        "fcT": c(np.transpose(L0_attn_fc_w)), "fcb": c(L0_attn_fc_b),
        "gamma": c(np.reshape(L0_xattn_gamma, (1,))),
        "wu": c(np.transpose(L0_ffn_W_up)), "wg": c(np.transpose(L0_ffn_W_gate)),
        "wd": c(np.transpose(L0_ffn_W_down)),
    }
    nc = bacc.Bacc("TRN2", target_bir_lowering=False, num_devices=1)
    args = [nc.dram_tensor("in_" + n, a.shape, mybir.dt.from_np(a.dtype), kind="ExternalInput").ap()
            for n, a in arrays.items()]
    result = nc.dram_tensor("result", x.shape, F32, kind="ExternalOutput").ap()
    decoder_layer(nc, *args, result)
    r = run_bass_kernel_spmd(nc, [{"in_" + n: a for n, a in arrays.items()}], core_ids=[0])
    return r.results[0]["result"]
```

```python
from contextlib import ExitStack

import concourse.bass as bass
from concourse import mybir

F32 = mybir.dt.float32
F16 = mybir.dt.float16
ACT = mybir.ActivationFunctionType
ALU = mybir.AluOpType
AXX = mybir.AxisListType.X
RMAX = bass.bass_isa.ReduceOp.max

P = 128
EPS_LN = 1e-5
EPS_Q = 1e-8


class Signal:

    def __init__(self, sem, per, by=1):
        self.sem, self.per, self.by = sem, per, by

    def at(self, batch, count):
        return (batch * self.per + count) * self.by


def decoder_layer(nc, x, xT, ctx_n, ctx_t, wq, wk, wv, fcT, fcb, gamma, wu, wg, wd, out):
    B, N, E = x.shape
    H = wq.shape[0]
    F = wu.shape[1]
    KT = E // P
    MT = N // P
    DH = 32
    XH = N // DH
    HG = P // DH
    FT = F // P
    PAIRS = FT // 2
    assert (E, N, XH, PAIRS, H, MT, KT) == (512, 256, 8, 8, 3, 2, 4)

    TOP = 1024.0
    DOWN = 2.0 ** -14
    WTOP = 4096.0
    QS = 64.0
    KTOP = 4096.0
    MROW = 4096.0
    X2S = 32.0
    HS = 2.0 ** -13
    ESC = 1.0 / (DOWN * TOP ** 3 * E ** 0.5)
    ASC = 1.0 / (DOWN * WTOP * H * TOP ** 2)
    XSC = 1.0 / (QS * KTOP * DH ** 0.5)
    DSC = 1.0 / (HS * X2S * X2S)

    BLOCKS = [("G", 0, 0), ("G", 0, 1), ("G", 1, 0), ("G", 1, 1), ("S", 0, 0), ("G", 2, 0), ("G", 2, 1),
              ("S", 1, 0), ("S", 2, 0)] + [("V", h, m) for h in range(H) for m in range(MT)]
    GV = [j for j, b in enumerate(BLOCKS) if b[0] != "S"]
    SB = [j for j, b in enumerate(BLOCKS) if b[0] == "S"]
    NBLK = len(BLOCKS)
    NGV = len(GV)
    TILES = XH * KT
    GT = TILES // MT
    S1_TURN = 12
    s1_of = {j: range(GT * j // S1_TURN, GT * (j + 1) // S1_TURN) if j < S1_TURN
             else range(*((0, 0) if j == S1_TURN else (GT + 2 * (j - S1_TURN) - 2, GT + 2 * (j - S1_TURN))))
             for j in range(NBLK)}
    XT = (12, 14)
    S1_BLOCKS = s1_of[NBLK - 1].stop
    S1_SLOTS = (TILES - S1_BLOCKS) // HG
    assert S1_BLOCKS + HG * S1_SLOTS == TILES and S1_SLOTS < KT

    with ExitStack() as ctx:
        def sb(name, shape, dt):
            return ctx.enter_context(nc.sbuf_tensor(name, shape, dt))

        def signal(name, per, by=1):
            return Signal(ctx.enter_context(nc.semaphore(name)), per, by)

        bank = {n: ctx.enter_context(nc.psum_tensor("bank_" + n, [P, 512], F32))
                for n in ("L0", "L1", "S0", "S1", "U", "G", "O", "T")}
        L = [bank["L0"], bank["L1"]]
        S = [bank["S0"], bank["S1"]]
        BANK = ([bank["U"], bank["G"]] + L) * 4
        BANK = BANK[:NBLK] + [L[1], L[0]]
        T16 = bank["T"][:, :].bitcast(F16)

        def s1_tiles(i, j):
            if isinstance(i, int) and i == 1:
                late = NBLK - S1_BLOCKS // 2
                return range(2 * (j - late), 2 * (j - late + 1)) if j >= late else range(0)
            return s1_of[j]

        def s1_banks(t, ffn):
            return S if t < S1_BLOCKS else [S[1]] if ffn else L + [S[1]]

        def s1_bank(t, ffn):
            banks = s1_banks(t, ffn)
            return banks[(t if t < S1_BLOCKS else t - S1_BLOCKS) % len(banks)]

        def s2_banks(ffn):
            return [S[0]] if ffn else [S[0], bank["U"], bank["G"]]

        A = sb("score_matrix", [P, 2, H, KT, E], F16)
        Bm = sb("value_matrix", [P, 2, H, KT, E], F16)
        Wu = sb("ternary_up", [P, KT, F], F16)
        Wg = sb("ternary_gate", [P, KT, F], F16)
        Wd = sb("ternary_down", [P, FT, E], F16)
        stage = sb("stage", [P, 1024], F32)
        xTs = sb("xT_split", [P, 2, KT, N], F16)
        xn = sb("x_rows", [P, MT, E], F32)
        work_a = sb("work_a", [P, 6144], F32)
        work_b = sb("work_b", [P, 6144], F32)
        work_c = sb("work_c", [P, 8192], F32)
        keys_t = sb("ctx_columns", [P, KT, N], F32)
        ksplit = sb("key_split", [P, 2, MT, E], F16)
        Gs = work_a[:, 0:2048].bitcast(F16).rearrange("p (b s k n) -> p b s k n", b=2, s=2, k=KT)
        Vs = work_a[:, 2048:5120].bitcast(F16).rearrange("p (s h m e) -> p s h m e", s=2, h=H, m=MT)
        we = work_a[:, 5120:6144].rearrange("p (b m n) -> p b m n", b=2, m=MT)
        den = work_a[:, 5120:5632]
        x1 = work_b[:, 0:1024].rearrange("p (m e) -> p m e", m=MT)
        hl = work_b[:, 1024:2048].bitcast(F16).rearrange("p (s m e) -> p s m e", s=2, m=MT)
        Qst = work_b[:, 2048:4096].bitcast(F16).rearrange("p (h e) -> p h e", h=XH)
        Kst = work_b[:, 4096:6144].bitcast(F16).rearrange("p (h e) -> p h e", h=XH)
        Pe = work_c[:, 0:2048].rearrange("p (v e) -> p v e", v=HG)
        Pe_too = work_c[:, 6144:8192].rearrange("p (v e) -> p v e", v=HG)
        Psum = work_c[:, 2048:4096].rearrange("p (v e) -> p v e", v=HG)
        x2 = work_c[:, 4096:5120].rearrange("p (m e) -> p m e", m=MT)
        x2T = work_c[:, 5120:6144].bitcast(F16).rearrange("p (s k n) -> p s k n", s=2, k=KT)
        hs = work_c[:, 6144:7168].bitcast(F16).rearrange("p (b s e n) -> p b s e n", b=2, s=2, e=2)
        th = work_c[:, 7168:8192].rearrange("p (b e) -> p b e", b=2)
        ws = sb("weight_split", [P, 2, H, MT, N], F16)
        fcb_b = sb("fcb_b", [P, E], F32)
        gam = sb("gam", [P, 1], F32)
        ones = sb("ones", [P, P], F32)
        id16 = sb("id16", [P, P], F16)
        id32 = sb("id32", [P, P], F32)
        mhalf = sb("mhalf", [P, MT], F32)
        eps = sb("eps", [P, MT], F32)
        nm = sb("neg_max_rows", [GT, MT, 2, P], F16)
        xmx = sb("cross_max", [P, TILES], F32)
        cm = sb("col_max", [P, H, MT], F32)
        nb = sb("exp_bias", [P, H, MT], F32)
        sm = sb("exp_sum", [P, H, MT], F32)
        rs = sb("exp_sum_inv", [P, H, MT], F32)
        r4 = sb("weight_scale", [P, H, MT], F32)
        bst = [sb(f"bn{r}", [P, MT, 6], F32) for r in range(3)]
        mv = [sb(f"mean_var{r}", [P, MT, 2], F32) for r in range(3)]
        ve = [sb(f"var_eps{r}", [P, MT], F32) for r in range(3)]
        rstd = [sb(f"rstd{r}", [P, MT], F32) for r in range(3)]
        sc = sb("scales", [P, 24], F32)
        (am_x, amr_x, inv_x, s_x, sq_x, esc, asc, am_c, amr_c, inv_c, s_c, xsc, c_esc, c_asc, am_w, amr_w,
         inv_w, s_w) = (sc[:, n:n + 1] for n in range(18))
        part = sb("abs_parts", [P, 3, 16], F32)
        tot = sb("abs_total", [P, 3], F32)
        wmax = sb("matrix_max", [P, 2, H], F32)
        mean_w = sb("weight_mean", [P, 3], F32)
        thr = sb("threshold", [P, 3], F32)
        nthr = sb("neg_threshold", [P, 3], F32)
        fsc = sb("ffn_scales", [P, 4], F32)
        half_u, gd, dsc = (fsc[:, n:n + 1] for n in range(3))

        wd_place = Wd[:, :, :].rearrange("p k e -> p (k e)").bitcast(F32)
        ring = [work_a[:, 0:2048], work_a[:, 2048:4096], work_a[:, 4096:6144],
                wd_place[:, 0:2048], wd_place[:, 2048:4096]]
        raw = [Bm[:, :, :, :, :].rearrange("p s h k e -> p (s h k e)").bitcast(F32), work_b[:, :]]
        stg = work_c[:, :].rearrange("p (c f) -> p c f", c=4)

        consts = signal("consts", 0)
        small_ld = signal("small_ld", 0, 16)
        w_ld = [signal(f"w_ld{n}", 0, 16) for n in range(5)]
        row_ld = [signal(f"row_ld{k}", 0, 16) for k in range(4)]
        ab_mm = signal("ab_mm", 0)
        ab_ev = signal("ab_ev", 0)
        f_ld = [signal(f"f_ld{n}", 0, 16) for n in range(4)]
        f_tot = signal("f_tot", 0)
        f_mm = signal("f_mm", 0)
        prep = signal("prep", 0)
        am_w_rdy = signal("am_w_rdy", 0)
        amr_w_rdy = signal("amr_w_rdy", 0)
        sw_rdy = signal("sw_rdy", 0)
        ab_hi = signal("ab_hi", 0)
        ab_lo = signal("ab_lo", 0)
        quant = signal("quant", 0)
        krow = signal("krow", 0)
        xT_ld = signal("xT_ld", 1, 16)
        am_x_rdy = signal("am_x_rdy", 1)
        amr_x_rdy = signal("amr_x_rdy", 1)
        xs_step = signal("xs_step", 5)
        xT_hi = signal("xT_hi", 1)
        xT_lo = signal("xT_lo", 1)
        xn_ld = signal("xn_ld", 1, 16)
        xb_rdy = signal("xb_rdy", 1)
        l_mm = signal("l_mm", NBLK + MT)
        gv_hi = signal("gv_hi", NGV)
        gv_lo = signal("gv_lo", NGV)
        cmax = signal("cmax", H)
        bias_rdy = signal("bias_rdy", H)
        e_done = signal("e_done", H)
        sum_inv = signal("sum_inv", H)
        wsc_rdy = signal("wsc_rdy", H)
        w_hi = signal("w_hi", H)
        w_lo = signal("w_lo", H)
        y1_rdy = signal("y1_rdy", MT)
        x1_rdy = signal("x1_rdy", 1)
        q_hi = signal("q_hi", 1)
        q_lo = signal("q_lo", 1)
        q_st = [signal(f"q_st{g}", 3 * HG, 16) for g in range(MT)]
        c_ld = signal("c_ld", 1, 16)
        am_c_rdy = signal("am_c_rdy", 1)
        amr_c_rdy = signal("amr_c_rdy", 1)
        cs_step = signal("cs_step", 3)
        k_hi = signal("k_hi", 1)
        k_lo = signal("k_lo", 1)
        k_st = [signal(f"k_st{g}", 3 * HG, 16) for g in range(MT)]
        ct_ld = signal("ct_ld", 1, 16)
        xsc_rdy = signal("xsc_rdy", 1)
        s1_mm = signal("s1_mm", TILES)
        s1_max = signal("s1_max", TILES)
        nt_mm = signal("nt_mm", MT)
        nm_hi = signal("nm_hi", MT)
        nm_lo = signal("nm_lo", MT)
        nm_st = signal("nm_st", 2 * MT, 16)
        s2_mm = signal("s2_mm", TILES)
        s2_exp = signal("s2_exp", TILES)
        p_add = signal("p_add", TILES)
        pv_mm = signal("pv_mm", 8)
        den_mm = signal("den_mm", MT)
        den_inv = signal("den_inv", 2 * MT)
        o_read = signal("o_read", MT)
        x1_copy = signal("x1_copy", 1)
        y2_rdy = signal("y2_rdy", MT)
        x2_rdy = signal("x2_rdy", 1)
        x2_hi = signal("x2_hi", 1)
        x2_lo = signal("x2_lo", 1)
        xt_mm = signal("xt_mm", 2)
        xt_ev = signal("xt_ev", 2)
        u_mm = signal("u_mm", PAIRS)
        g_mm = signal("g_mm", PAIRS)
        th_rdy = signal("th_rdy", PAIRS)
        t_rdy = signal("t_rdy", PAIRS)
        p_rdy = signal("p_rdy", PAIRS)
        h_hi = signal("h_hi", PAIRS)
        h_lo = signal("h_lo", PAIRS)
        dn_mm = signal("dn_mm", PAIRS)
        y3_rdy = signal("y3_rdy", MT)
        out_rdy = signal("out_rdy", 1)
        out_st = signal("out_st", 1, 16)
        ln_st = [signal(f"ln_st{r}", MT) for r in range(3)]
        ln_ag = [signal(f"ln_ag{r}", MT) for r in range(3)]
        ln_ve = [signal(f"ln_ve{r}", 1) for r in range(3)]
        ln_rs = [signal(f"ln_rs{r}", 1) for r in range(3)]

        block = ctx.enter_context(nc.Block())

        pause, pause_x, pause_c = (sc[:, n:n + 1] for n in (18, 19, 20))

        def run_stages(eng, stage_of):
            flags = lambda i: (i < B, 1 <= i <= B, 2 <= i <= B + 1, i + 1 < B, i >= 3)
            for i in range(3):
                stage_of(i, *flags(i))
            with eng.Fori(3, B - 1) as i:
                stage_of(i, *flags(3))
            for i in range(B - 1, B + 3):
                stage_of(i, *flags(i))

        def exp_tiles(u, ffn):
            return Pe if ffn or u % 2 == 0 else Pe_too

        SEQ = [(wq, 0), (wk, 0), (wq, 1), (wk, 1), (wq, 2), (wk, 2), (fcT, None), (wv, 0), (wv, 1), (wv, 2)]
        SLOT = [0, 1, 2, 3, 4, 0, 1, 2, 3, 4]
        whole_loads = lambda n: SLOT[2:n + 1].count(SLOT[n])
        SLOT_READ = {5: KT, 6: KT, 7: 2 * KT, 8: 2 * KT, 9: 3 * KT}
        B_SPLIT = (2, 3, 4)
        QUANTIZE = (0, 1, 3, 5)
        F_SUM = (7, 18)
        ring_of = lambda n: ring[SLOT[n]]

        @block.sync
        def _(sp):
            def load_w(n):
                w, h = SEQ[n]
                src = (w[h] if h is not None else w).rearrange("(k p) e -> p k e", p=P)
                if n in SLOT_READ:
                    sp.wait_ge(ab_mm.sem, ab_mm.at(0, SLOT_READ[n]))
                sp.dma_start(ring_of(n)[:, :].rearrange("p (k e) -> p k e", k=KT), src).then_inc(
                    w_ld[SLOT[n]].sem, 16)

            def load_f(m, c):
                src = [wu, wg, wd][m].rearrange("(k p) f -> p k f", p=P)
                if m:
                    sp.wait_ge(quant.sem, quant.at(0, 4 * (m - 1) + c + 1))
                if m < 2:
                    sp.dma_start(stg[:, c, :], src[:, c, :]).then_inc(f_ld[c].sem, 16)
                else:
                    sp.dma_start(stg[:, c, :].rearrange("p (k e) -> p k e", e=E),
                                 src[:, 4 * c:4 * c + 4, :]).then_inc(f_ld[c].sem, 16)

            for k in range(KT):
                for n in range(2):
                    sp.dma_start(ring_of(n)[:, k * E:(k + 1) * E],
                                 SEQ[n][0][0, k * P:(k + 1) * P, :]).then_inc(row_ld[k].sem, 16)
            sp.dma_start(stage[:, :].rearrange("p (k n) -> p k n", k=KT),
                         xT[0].rearrange("(k p) n -> p k n", p=P)).then_inc(xT_ld.sem, 16)
            for n in range(2, 4):
                load_w(n)
            for c in range(4):
                load_f(0, c)
            for n in range(4, 10):
                load_w(n)
            sp.dma_start(fcb_b[:, :], fcb.partition_broadcast(P)).then_inc(small_ld.sem, 16)
            sp.dma_start(gam[:, :], gamma.partition_broadcast(P)).then_inc(small_ld.sem, 16)
            for c in range(4):
                load_f(1, c)
            for c in range(4):
                load_f(2, c)

            def stages(i, att, cross, ffn, nxt, last_out):
                b, f = i - 1, i - 2
                if cross:
                    sp.wait_ge(consts.sem, 7)
                    sp.wait_ge(pv_mm.sem, pv_mm.at(b - 1, 8))
                    sp.dma_start(keys_t[:, :, :], ctx_t[b].rearrange("(k p) n -> p k n", p=P)).then_inc(
                        ct_ld.sem, 16)
                if att:
                    sp.wait_ge(consts.sem, 7)
                    sp.wait_ge(xT_lo.sem, xT_lo.at(i, 1))
                    sp.dma_start(stage[:, :].rearrange("p (m e) -> p m e", m=MT),
                                 ctx_n[i].rearrange("(m p) e -> p m e", p=P)).then_inc(c_ld.sem, 16)
                if last_out:
                    sp.wait_ge(consts.sem, 7)
                    sp.wait_ge(out_rdy.sem, out_rdy.at(i - 3, 1))
                    sp.dma_start(out[i - 3].rearrange("(m p) e -> p m e", p=P), x2[:, :, :]).then_inc(
                        out_st.sem, 16)
                if att:
                    sp.wait_ge(consts.sem, 7)
                    sp.wait_ge(x1_copy.sem, x1_copy.at(i - 1, 1))
                    sp.dma_start(xn[:, :, :], x[i].rearrange("(m p) e -> p m e", p=P)).then_inc(xn_ld.sem, 16)
                if nxt:
                    sp.wait_ge(consts.sem, 7)
                    sp.wait_ge(k_lo.sem, k_lo.at(i, 1))
                    sp.dma_start(stage[:, :].rearrange("p (k n) -> p k n", k=KT),
                                 xT[i + 1].rearrange("(k p) n -> p k n", p=P)).then_inc(xT_ld.sem, 16)
                if cross:
                    for grp in range(MT):
                        for s in range(2):
                            rdy = (nm_hi, nm_lo)[s]
                            sp.wait_ge(rdy.sem, rdy.at(b, grp + 1))
                            sp.dma_start(Qst[96 + s:97 + s, HG * grp:HG * (grp + 1), :].rearrange(
                                "p h (t c) -> p (h t) c", c=P), nm[:, grp, s, :]).then_inc(nm_st.sem, 16)
                if att:
                    keys = [(grp, ksplit, Kst, (0, 0, 1), k_st[grp], k_lo) for grp in range(MT)]
                    queries = [(grp, hl, Qst, (0, 1, 0), q_st[grp], q_lo) for grp in range(MT)]
                    moves = ([keys[0], queries[0], keys[1], queries[1]] if cross
                             else keys + queries)
                    for grp, src, dst, order, done, rdy in moves:
                        if cross and src is ksplit:
                            sp.wait_ge(s2_mm.sem, s2_mm.at(b, GT * (grp + 1)))
                        sp.wait_ge(rdy.sem, rdy.at(i, 1))
                        for j, s in enumerate(order):
                            for hd in range(HG):
                                sp.dma_start(dst[32 * j:32 * j + 32, HG * grp + hd, :],
                                             src[32 * hd:32 * hd + 32, s, grp, :]).then_inc(done.sem, 16)

            run_stages(sp, stages)
            sp.wait_ge(consts.sem, 7)
            sp.wait_ge(out_st.sem, out_st.at(B - 1, 1))

        @block.gpsimd
        def _(pool):
            g = nc.gpsimd
            g.memset(ones[:, :], 1.0).then_inc(consts.sem, 1)
            g.memset(mhalf[:, :], -0.5).then_inc(consts.sem, 1)
            g.memset(eps[:, :], EPS_LN).then_inc(consts.sem, 1)
            g.memset(id16[:, :], 0.0).then_inc(consts.sem, 1)
            g.memset(id32[:, :], 0.0).then_inc(consts.sem, 1)
            pool.wait_ge(consts.sem, consts.at(0, 5))
            for t in (id16, id32):
                g.affine_select(out=t[:, :], in_=t[:, :], compare_op=ALU.not_equal, fill=1.0, base=0,
                                pattern=[[-1, P]], channel_multiplier=1).then_inc(consts.sem, 1)

            def all_max(rdy, done, dst, src, b, k=1):
                pool.wait_ge(rdy.sem, rdy.at(b, k))
                if not isinstance(b, int):
                    g.tensor_tensor(pause_c if rdy is am_c_rdy else pause_x, mhalf[:, 0:1], mhalf[:, 0:1],
                                    ALU.add)
                g.partition_all_reduce(dst, src, P, RMAX).then_inc(done.sem, 1)

            def rstd_of(r, b):
                pool.wait_ge(ln_ag[r].sem, ln_ag[r].at(b, MT))
                g.tensor_tensor(ve[r][:, :], mv[r][:, :, 1], eps[:, :], ALU.add).then_inc(ln_ve[r].sem, 1)
                pool.wait_ge(ln_ve[r].sem, ln_ve[r].at(b, 1))
                g.tensor_tensor(rstd[r][:, :], ve[r][:, :], mhalf[:, :], ALU.pow).then_inc(ln_rs[r].sem, 1)

            all_max(am_x_rdy, amr_x_rdy, amr_x, am_x, 0)
            all_max(am_w_rdy, amr_w_rdy, amr_w, am_w, 0, 1)
            all_max(am_w_rdy, amr_w_rdy, amr_w, am_w, 0, 2)
            pool.wait_ge(ab_lo.sem, ab_lo.at(0, 2 * H))
            g.memset(Kst[96:98, :, :], MROW).then_inc(krow.sem, 1)
            pool.wait_ge(krow.sem, krow.at(0, 1))
            pool.wait_ge(small_ld.sem, small_ld.at(0, 2))

            def stages(i, att, cross, ffn, nxt, last_out):
                b, f = i - 1, i - 2

                def add_tiles(u):
                    for v in range(HG):
                        n = u * HG + v
                        pool.wait_ge(s2_exp.sem, s2_exp.at(b, n + 1))
                        if u % KT == 0:
                            if v == 0:
                                pool.wait_ge(den_mm.sem, den_mm.at(b, u // KT))
                            g.tensor_tensor(Psum[:, v, :], exp_tiles(u, ffn)[:, v, :],
                                            ones[:, 0:1].to_broadcast([P, E]), ALU.mult).then_inc(p_add.sem, 1)
                        else:
                            pool.wait_ge(p_add.sem, p_add.at(b, n - HG + 1))
                            g.tensor_tensor(Psum[:, v, :], Psum[:, v, :], exp_tiles(u, ffn)[:, v, :],
                                            ALU.add).then_inc(p_add.sem, 1)

                if last_out:
                    rstd_of(2, i - 3)
                if ffn:
                    rstd_of(1, f)
                if att:
                    all_max(am_c_rdy, amr_c_rdy, amr_c, am_c, i)
                    pool.wait_ge(xn_ld.sem, xn_ld.at(i, 1))
                    g.tensor_tensor(xn[:, :, :], xn[:, :, :],
                                    fcb_b[:, :].rearrange("p (a e) -> p a e", a=1).to_broadcast([P, MT, E]),
                                    ALU.add).then_inc(xb_rdy.sem, 1)
                if nxt and not cross:
                    all_max(am_x_rdy, amr_x_rdy, amr_x, am_x, i + 1)
                for u in range(8):
                    if u == 2 and att:
                        rstd_of(0, i)
                    if u == 5 and nxt and cross:
                        all_max(am_x_rdy, amr_x_rdy, amr_x, am_x, i + 1)
                    if cross and (ffn or u < S1_SLOTS):
                        add_tiles(u)

            run_stages(pool, stages)

        @block.scalar
        def _(act):
            a = nc.scalar

            def split_hi(dst, n, h):
                act.wait_ge(sw_rdy.sem, sw_rdy.at(0, n + 1))
                if n:
                    act.wait_ge(ab_lo.sem, ab_lo.at(0, H))
                a.activation(dst[:, 0, h].rearrange("p k e -> p (k e)"), raw[n][:, h * KT * E:(h + 1) * KT * E],
                             ACT.Copy, scale=s_w).then_inc(ab_hi.sem, 1)

            def xT_split_hi(b):
                act.wait_ge(xs_step.sem, xs_step.at(b, 3))
                a.activation(xTs[:, 0].rearrange("p k n -> p (k n)"), stage[:, :], ACT.Copy,
                             scale=s_x).then_inc(xT_hi.sem, 1)

            for t in range(2 * H * KT):
                n, row = t // (H * KT), t % (H * KT)
                act.wait_ge(ab_mm.sem, ab_mm.at(0, t + 1))
                a.activation(raw[n][:, row * E:(row + 1) * E], BANK[t % 4][:, :], ACT.Copy).then_inc(ab_ev.sem, 1)
                if t == H * KT:
                    xT_split_hi(0)
                    for h in range(H):
                        split_hi(A, 0, h)

            def stages(i, att, cross, ffn, nxt, last_out):
                b, f = i - 1, i - 2

                def weight_hi(h):
                    act.wait_ge(wsc_rdy.sem, wsc_rdy.at(i, h + 1))
                    for m in range(MT):
                        last = a.activation(ws[:, 0, h, m, :], we[:, h % 2, m, :], ACT.Copy,
                                            scale=r4[:, h, m:m + 1])
                    last.then_inc(w_hi.sem, 1)

                for j, (kind, h, m) in enumerate(BLOCKS):
                    if isinstance(i, int) and i == 0 and j in B_SPLIT:
                        split_hi(Bm, 1, B_SPLIT.index(j))
                    if att:
                        act.wait_ge(l_mm.sem, l_mm.at(i, j + 1))
                        if kind == "S":
                            act.wait_ge(bias_rdy.sem, bias_rdy.at(i, h + 1))
                            if h == 2:
                                act.wait_ge(w_lo.sem, w_lo.at(i, 1))
                            for mt in range(MT):
                                last = a.activation(we[:, h % 2, mt, :], BANK[j][:, mt * N:mt * N + N], ACT.Exp,
                                                    bias=nb[:, h, mt:mt + 1], scale=esc,
                                                    accum_out=sm[:, h, mt:mt + 1])
                            last.then_inc(e_done.sem, 1)
                        else:
                            dst = (Gs[:, h % 2, 0, 2 * m:2 * m + 2, :].rearrange("p k n -> p (k n)")
                                   if kind == "G" else Vs[:, 0, h, m, :])
                            a.activation(dst, BANK[j][:, :], ACT.Copy, scale=DOWN).then_inc(gv_hi.sem, 1)
                        if j - 1 in SB:
                            weight_hi(SB.index(j - 1))
                    if ffn and j == 10:
                        act.wait_ge(x2_rdy.sem, x2_rdy.at(f, 1))
                        if cross:
                            for grp in range(MT):
                                act.wait_ge(q_st[grp].sem, q_st[grp].at(b, 3 * HG))
                        a.activation(hl[:, 0].rearrange("p m e -> p (m e)"),
                                     x2[:, :, :].rearrange("p m e -> p (m e)"), ACT.Copy,
                                     scale=X2S).then_inc(x2_hi.sem, 1)
                    if cross and j == 10:
                        act.wait_ge(q_lo.sem, q_lo.at(b, 1))
                        a.activation(x1[:, :, :].rearrange("p m e -> p (m e)"),
                                     xn[:, :, :].rearrange("p m e -> p (m e)"), ACT.Copy).then_inc(x1_copy.sem, 1)
                    if att and j == 11:
                        act.wait_ge(cs_step.sem, cs_step.at(i, 3))
                        for grp in range(MT):
                            act.wait_ge(k_st[grp].sem, k_st[grp].at(i - 1, 3 * HG))
                        a.activation(ksplit[:, 0].rearrange("p m e -> p (m e)"), stage[:, :], ACT.Copy,
                                     scale=s_c).then_inc(k_hi.sem, 1)
                    if ffn and j in XT:
                        s = XT.index(j)
                        act.wait_ge(xt_mm.sem, xt_mm.at(f, s + 1))
                        a.activation(x2T[:, s].rearrange("p k n -> p (k n)"), T16, ACT.Copy).then_inc(
                            xt_ev.sem, 1)

                def exps(u, v):
                    n = u * HG + v
                    act.wait_ge(s2_mm.sem, s2_mm.at(b, n + 1))
                    held = HG if ffn else 2 * HG
                    if n >= held:
                        act.wait_ge(p_add.sem, p_add.at(b, n - held + 1))
                    banks = s2_banks(ffn)
                    a.activation(exp_tiles(u, ffn)[:, v, :], banks[n % len(banks)][:, :], ACT.Exp,
                                 scale=xsc).then_inc(s2_exp.sem, 1)

                def hidden_hi(u):
                    act.wait_ge(p_rdy.sem, p_rdy.at(f, u + 1))
                    a.activation(hs[:, u % 2, 0].rearrange("p e n -> p (e n)"), th[:, u % 2, :],
                                 ACT.Copy).then_inc(h_hi.sem, 1)

                if nxt and not cross:
                    act.wait_ge(l_mm.sem, l_mm.at(i, NBLK))
                    xT_split_hi(i + 1)
                for u in range(8):
                    if cross:
                        if u == 0:
                            act.wait_ge(xsc_rdy.sem, xsc_rdy.at(b, 1))
                        exps(u, 0)
                    if ffn and u:
                        hidden_hi(u - 1)
                    if cross:
                        exps(u, 1)
                    if ffn:
                        act.wait_ge(u_mm.sem, u_mm.at(f, u + 1))
                        a.activation(th[:, u % 2, :], bank["U"][:, :], ACT.Tanh, scale=half_u).then_inc(
                            th_rdy.sem, 1)
                    if cross:
                        exps(u, 2)
                        exps(u, 3)
                    if u == 2 and att:
                        act.wait_ge(x1_rdy.sem, x1_rdy.at(i, 1))
                        if ffn:
                            act.wait_ge(xt_mm.sem, xt_mm.at(f, 2))
                        a.activation(hl[:, 0].rearrange("p m e -> p (m e)"),
                                     xn[:, :, :].rearrange("p m e -> p (m e)"), ACT.Copy,
                                     scale=QS).then_inc(q_hi.sem, 1)
                    if u == 6 and nxt and cross:
                        xT_split_hi(i + 1)
                if ffn:
                    hidden_hi(PAIRS - 1)

            run_stages(act, stages)

        @block.tensor
        def _(pe):
            t_ = nc.tensor
            pe.wait_ge(consts.sem, consts.at(0, 7))

            def abs_sum(m):
                pe.wait_ge(f_tot.sem, f_tot.at(0, m + 1))
                t_.matmul(bank["O"][:, m:m + 1], ones[:, :], tot[:, m:m + 1], start=True,
                          stop=True).then_inc(f_mm.sem, 1)

            for t in range(2 * H * KT):
                h, et = t // KT % H, t % KT
                if t < H * KT:
                    nl, nr = 2 * h, 2 * h + 1
                else:
                    nl, nr = 7 + h, 6
                if t and et == 0:
                    for n in (nl, nr):
                        pe.wait_ge(w_ld[SLOT[n]].sem, w_ld[SLOT[n]].at(0, whole_loads(n)))
                if t >= 4:
                    pe.wait_ge(ab_ev.sem, ab_ev.at(0, t - 3))
                lhs = ring_of(nl).rearrange("p (k e) -> p k e", k=KT)
                rhs = ring_of(nr).rearrange("p (k e) -> p k e", k=KT)
                for k in range(KT):
                    if t == 0:
                        pe.wait_ge(row_ld[k].sem, row_ld[k].at(0, 2))
                    last = t_.matmul(BANK[t % 4][:, :], lhs[:, k, et * P:(et + 1) * P], rhs[:, k, :],
                                     start=(k == 0), stop=(k == KT - 1))
                last.then_inc(ab_mm.sem, 1)
                if t in F_SUM:
                    abs_sum(F_SUM.index(t))

            def split_products(dst, terms, between=None):
                for n, (lhs, rhs) in enumerate(terms):
                    if between and n == len(terms) // 2:
                        between()
                    last = t_.matmul(dst, lhs, rhs, start=(n == 0), stop=(n == len(terms) - 1))
                return last

            PARTS = ((0, 0), (0, 1), (1, 0))

            def stages(i, att, cross, ffn, nxt, last_out):
                b, f = i - 1, i - 2

                def s1(t):
                    h, qt = t // KT, t % KT
                    if t % GT == 0:
                        grp = t // GT
                        pe.wait_ge(q_st[grp].sem, q_st[grp].at(b, 3 * HG))
                        pe.wait_ge(k_st[grp].sem, k_st[grp].at(b, 3 * HG))
                    if t == 0:
                        pe.wait_ge(s2_exp.sem, s2_exp.at(b - 1, TILES))
                        pe.wait_ge(s1_max.sem, s1_max.at(b - 1, TILES))
                    else:
                        turns = len(s1_banks(t, ffn))
                        if t >= turns:
                            pe.wait_ge(s1_max.sem, s1_max.at(b, t + 1 - turns))
                        if t == S1_BLOCKS and att and not ffn:
                            pe.wait_ge(y1_rdy.sem, y1_rdy.at(i, MT))
                    t_.matmul(s1_bank(t, ffn)[:, :], Qst[0:96, h, qt * P:(qt + 1) * P], Kst[0:96, h, :], start=True,
                              stop=True).then_inc(s1_mm.sem, 1)

                def max_rows(grp):
                    pe.wait_ge(s1_max.sem, s1_max.at(b, GT * (grp + 1)))
                    if ffn:
                        pe.wait_ge(xt_ev.sem, xt_ev.at(f, grp + 1))
                    t_.transpose(bank["T"][0:GT, 0:P], xmx[:, GT * grp:GT * (grp + 1)],
                                 id32[:, :]).then_inc(nt_mm.sem, 1)

                def denom(batch, grp):
                    pe.wait_ge(p_add.sem, p_add.at(batch, (grp + 1) * GT))
                    pe.wait_ge(nm_lo.sem, nm_lo.at(batch, MT))
                    for v in range(HG):
                        last = t_.matmul(bank["T"][v * DH:(v + 1) * DH, :], ones[:, 0:DH], Psum[:, v, :],
                                         start=True, stop=True, skip_group_check=True)
                    last.then_inc(den_mm.sem, 1)

                for j, (kind, h, m) in enumerate(BLOCKS):
                    pend = list(s1_tiles(i, j)) if cross else []

                    def s1_next():
                        if pend:
                            s1(pend.pop(0))

                    if att:
                        bk = BANK[j]
                        if j == 0:
                            pe.wait_ge(xT_lo.sem, xT_lo.at(i, 1))
                            if isinstance(i, int) and i == 0:
                                pe.wait_ge(ab_lo.sem, ab_lo.at(0, H))
                                pe.wait_ge(ab_ev.sem, ab_ev.at(0, 2 * H * KT))
                        if kind == "V" and isinstance(i, int) and i == 0:
                            pe.wait_ge(ab_lo.sem, ab_lo.at(0, H + h + 1))
                        if j < 2:
                            if ffn:
                                rdy = (t_rdy, p_rdy)[j]
                                pe.wait_ge(rdy.sem, rdy.at(f - 1, PAIRS))
                        elif j < 4:
                            if ffn:
                                pe.wait_ge(y3_rdy.sem, y3_rdy.at(f - 1, MT))
                            pe.wait_ge(y1_rdy.sem, y1_rdy.at(i - 1, MT))
                        elif (j - 4) in SB:
                            pe.wait_ge(e_done.sem, e_done.at(i, SB.index(j - 4) + 1))
                        else:
                            pe.wait_ge(gv_lo.sem, gv_lo.at(i, GV.index(j - 4) + 1))
                        if kind == "G":
                            for c in range(2):
                                cols = slice((2 * m + c) * P, (2 * m + c + 1) * P)
                                last = split_products(bk[:, c * N:(c + 1) * N], [
                                    (A[:, pl, h, k, cols], xTs[:, pr, k, :]) for pl, pr in PARTS for k in range(KT)])
                                if c == 0:
                                    s1_next()
                        elif kind == "S":
                            pe.wait_ge(gv_lo.sem, gv_lo.at(i, GV.index(BLOCKS.index(("G", h, 1))) + 1))
                            for c in range(MT):
                                last = split_products(bk[:, c * N:(c + 1) * N], [
                                    (xTs[:, pl, k, c * P:(c + 1) * P], Gs[:, h % 2, pr, k, :])
                                    for pl, pr in PARTS for k in range(KT)])
                                if c == 0:
                                    s1_next()
                        else:
                            last = split_products(bk[:, :], [
                                (xTs[:, pl, k, m * P:(m + 1) * P], Bm[:, pr, h, k, :])
                                for pl, pr in PARTS for k in range(KT)], s1_next)
                        last.then_inc(l_mm.sem, 1)
                    while pend:
                        s1_next()
                    if isinstance(i, int) and i == 0 and j == 12:
                        abs_sum(2)
                    if ffn and j == 0:
                        denom(f, 1)
                    if cross and j == S1_TURN + 1:
                        max_rows(0)
                    if ffn and j in XT:
                        s = XT.index(j)
                        rdy = (x2_hi, x2_lo)[s]
                        pe.wait_ge(rdy.sem, rdy.at(f, 1))
                        if s == 0:
                            pe.wait_ge(den_inv.sem, den_inv.at(f, 2 * MT))
                        else:
                            pe.wait_ge(xt_ev.sem, xt_ev.at(f, 1))
                            if cross:
                                pe.wait_ge(nm_lo.sem, nm_lo.at(b, 1))
                        for k in range(KT):
                            for mt in range(MT):
                                c0 = k * N + mt * P
                                last = t_.transpose(T16[:, c0:c0 + P], hl[:, s, mt, k * P:(k + 1) * P], id16[:, :])
                        last.then_inc(xt_mm.sem, 1)
                if att:
                    pe.wait_ge(w_lo.sem, w_lo.at(i, H))
                    pe.wait_ge(gv_lo.sem, gv_lo.at(i, NGV - 1))
                    for n in range(MT):
                        j = NBLK + n
                        for h in range(H):
                            for m in range(MT):
                                if (h, m) == (H - 1, MT - 1):
                                    pe.wait_ge(gv_lo.sem, gv_lo.at(i, NGV))
                                for pl, pr in PARTS:
                                    last = t_.matmul(BANK[j][:, :], ws[:, pl, h, m, n * P:(n + 1) * P],
                                                     Vs[:, pr, h, m, :], start=(h == m == pl == pr == 0),
                                                     stop=(h == H - 1 and m == MT - 1 and pl == 1))
                        last.then_inc(l_mm.sem, 1)

                def s2(u, v):
                    n = u * HG + v
                    h, lt = HG * (u // KT) + v, u % KT
                    if n % GT == 0:
                        pe.wait_ge(nm_st.sem, nm_st.at(b, 2 * (n // GT + 1)))
                        pe.wait_ge(krow.sem, krow.at(0, 1))
                    banks = s2_banks(ffn)
                    if n >= len(banks):
                        pe.wait_ge(s2_exp.sem, s2_exp.at(b, n + 1 - len(banks)))
                    if n == 0:
                        pe.wait_ge(s1_max.sem, s1_max.at(b, S1_BLOCKS))
                    t_.matmul(banks[n % len(banks)][:, :], Kst[0:98, h, lt * P:(lt + 1) * P], Qst[0:98, h, :],
                              start=True, stop=True).then_inc(s2_mm.sem, 1)

                def hidden(u, W, dst, done, free):
                    for e in range(2):
                        v = 2 * (dst is bank["G"]) + e
                        if ffn:
                            if e == 0:
                                pe.wait_ge(free.sem, free.at(f, u))
                            cols = slice((2 * u + e) * P, (2 * u + e + 1) * P)
                        for s in range(2):
                            if ffn:
                                for k in range(KT):
                                    last = t_.matmul(dst[:, e * N:(e + 1) * N], W[:, k, cols], x2T[:, s, k, :],
                                                     start=(s == 0 and k == 0), stop=(s == 1 and k == KT - 1))
                                if e == 1 and s == 1:
                                    last.then_inc(done.sem, 1)
                            if cross and s == 0:
                                s2(u, v)
                            if cross and s == 1 and u < S1_SLOTS:
                                s1(S1_BLOCKS + HG * u + v)

                def down(u):
                    pe.wait_ge(h_lo.sem, h_lo.at(f, u + 1))
                    if u == 0:
                        if att:
                            pe.wait_ge(y1_rdy.sem, y1_rdy.at(i, MT))
                        pe.wait_ge(y3_rdy.sem, y3_rdy.at(f - 1, MT))
                    for n in range(MT):
                        for e in range(2):
                            for s in range(2):
                                last = t_.matmul(L[n][:, :], hs[:, u % 2, s, e, n * P:(n + 1) * P],
                                                 Wd[:, 2 * u + e, :], start=(u == 0 and e == 0 and s == 0),
                                                 stop=(u == PAIRS - 1 and e == 1 and s == 1))
                    last.then_inc(dn_mm.sem, 1)

                def pv(u):
                    grp, lt = u // KT, u % KT
                    if u == 0:
                        pe.wait_ge(ct_ld.sem, ct_ld.at(b, 1))
                    if lt == 0:
                        pe.wait_ge(o_read.sem, o_read.at(b, grp))
                    pe.wait_ge(s2_exp.sem, s2_exp.at(b, HG * (u + 1)))
                    for v in range(HG):
                        c0 = grp * P + v * DH
                        last = t_.matmul(bank["O"][v * DH:(v + 1) * DH, :], keys_t[:, lt, c0:c0 + DH],
                                         exp_tiles(u, ffn)[:, v, :],
                                         start=(lt == 0), stop=(lt == KT - 1), skip_group_check=True)
                    last.then_inc(pv_mm.sem, 1)

                if ffn:
                    pe.wait_ge(xt_ev.sem, xt_ev.at(f, 2))
                if cross and not ffn:
                    ahead = len(s2_banks(ffn))
                    for n in range(TILES + ahead):
                        if n < TILES:
                            s2(n // HG, n % HG)
                        if n < HG * S1_SLOTS:
                            s1(S1_BLOCKS + n)
                        if n == HG * S1_SLOTS:
                            max_rows(1)
                        if n >= ahead and (n - ahead) % HG == HG - 1:
                            pv((n - ahead) // HG)
                        if n - ahead == GT - 1:
                            denom(b, 0)
                for u in range(8 if ffn else 0):
                    if u == KT and cross:
                        denom(b, 0)
                    hidden(u, Wu, bank["U"], u_mm, t_rdy)
                    hidden(u, Wg, bank["G"], g_mm, p_rdy)
                    if ffn and u:
                        down(u - 1)
                    if cross:
                        if u == S1_SLOTS - 1:
                            max_rows(1)
                        pv(u)
                if ffn:
                    down(PAIRS - 1)

            run_stages(pe, stages)

        @block.vector
        def _(dve):
            v_ = nc.vector
            steps = [0]

            def step(ins):
                steps[0] += 1
                ins.then_inc(prep.sem, 1)
                dve.wait_ge(prep.sem, prep.at(0, steps[0]))

            def x_absmax(b):
                dve.wait_ge(xT_ld.sem, xT_ld.at(b, 1))
                v_.tensor_reduce(am_x, stage[:, :], AXX, ALU.max, apply_absolute_value=True).then_inc(
                    am_x_rdy.sem, 1)

            def x_scales(b):
                dve.wait_ge(amr_x_rdy.sem, amr_x_rdy.at(b, 1))
                v_.tensor_scalar(amr_x, amr_x, 1e-30, None, ALU.max).then_inc(xs_step.sem, 1)
                dve.wait_ge(xs_step.sem, xs_step.at(b, 1))
                v_.reciprocal(inv_x, amr_x).then_inc(xs_step.sem, 1)
                dve.wait_ge(xs_step.sem, xs_step.at(b, 2))
                v_.tensor_scalar(s_x, inv_x, TOP, None, ALU.mult).then_inc(xs_step.sem, 1)

            def x_scales_back():
                v_.scalar_tensor_tensor(esc, amr_x, amr_x, c_esc, ALU.mult, ALU.mult).then_inc(xs_step.sem, 1)
                v_.tensor_tensor(asc, amr_x, c_asc, ALU.mult).then_inc(xs_step.sem, 1)

            def x_lo(b):
                dve.wait_ge(xT_hi.sem, xT_hi.at(b, 1))
                v_.scalar_tensor_tensor(xTs[:, 1].rearrange("p k n -> p (k n)"), stage[:, :], s_x,
                                        xTs[:, 0].rearrange("p k n -> p (k n)"), ALU.mult,
                                        ALU.subtract).then_inc(xT_lo.sem, 1)

            def matrix_part(n, h):
                dve.wait_ge(ab_ev.sem, ab_ev.at(0, (n * H + h + 1) * KT))
                return v_.tensor_reduce(wmax[:, n, h:h + 1], raw[n][:, h * KT * E:(h + 1) * KT * E], AXX, ALU.max,
                                        apply_absolute_value=True)

            def matrix_max(n):
                for h in range(2 * (1 - n), H):
                    last = matrix_part(n, h)
                step(last)
                v_.tensor_reduce(am_w, wmax[:, n, :], AXX, ALU.max).then_inc(am_w_rdy.sem, 1)

            def matrix_scale(n, back, const):
                dve.wait_ge(amr_w_rdy.sem, amr_w_rdy.at(0, n + 1))
                step(v_.tensor_scalar(amr_w, amr_w, 1e-30, None, ALU.max))
                step(v_.reciprocal(inv_w, amr_w))
                step(v_.tensor_scalar(back, amr_w, const, None, ALU.mult))
                v_.tensor_scalar(s_w, inv_w, TOP, None, ALU.mult).then_inc(sw_rdy.sem, 1)

            def matrix_lo(dst, n, h):
                dve.wait_ge(ab_hi.sem, ab_hi.at(0, n * H + h + 1))
                v_.scalar_tensor_tensor(dst[:, 1, h].rearrange("p k e -> p (k e)"),
                                        raw[n][:, h * KT * E:(h + 1) * KT * E], s_w,
                                        dst[:, 0, h].rearrange("p k e -> p (k e)"), ALU.mult,
                                        ALU.subtract).then_inc(ab_lo.sem, 1)

            def abs_part(m, c):
                dve.wait_ge(f_ld[c].sem, f_ld[c].at(0, m + 1))
                return v_.tensor_reduce(part[:, m, 4 * c:4 * c + 4],
                                        stg[:, c, :].rearrange("p (q e) -> p q e", e=E), AXX, ALU.add,
                                        apply_absolute_value=True)

            def abs_total(m):
                v_.tensor_reduce(tot[:, m:m + 1], part[:, m, :], AXX, ALU.add).then_inc(f_tot.sem, 1)

            def threshold(m):
                dve.wait_ge(f_mm.sem, f_mm.at(0, m + 1))
                step(v_.tensor_scalar(mean_w[:, m:m + 1], bank["O"][:, m:m + 1], 1.0 / (E * F), EPS_Q, ALU.mult,
                                      ALU.add))
                step(v_.tensor_scalar(thr[:, m:m + 1], mean_w[:, m:m + 1], 0.5, None, ALU.mult))
                step(v_.tensor_scalar(nthr[:, m:m + 1], mean_w[:, m:m + 1], -0.5, None, ALU.mult))

            def quantize(m, c):
                W = [Wu, Wg, Wd][m]
                dst = W[:, c, :] if m < 2 else W[:, 4 * c:4 * c + 4, :].rearrange("p k e -> p (k e)")
                step(v_.tensor_scalar(dst, stg[:, c, :], nthr[:, m:m + 1], None, ALU.is_lt))
                v_.scalar_tensor_tensor(dst, stg[:, c, :], thr[:, m:m + 1], dst, ALU.is_gt,
                                        ALU.subtract).then_inc(quant.sem, 1)

            def ln_stats(r, b, src, m):
                v_.bn_stats(bst[r][:, m, :], src[:, m, :]).then_inc(ln_st[r].sem, 1)
                if m == MT - 1:
                    dve.wait_ge(ln_st[r].sem, ln_st[r].at(b, MT))
                    v_.memset(pause, 0.0)
                    for n in range(MT):
                        v_.bn_aggr(mv[r][:, n, :], bst[r][:, n, :]).then_inc(ln_ag[r].sem, 1)

            def ln_apply(r, b, dst, src):
                dve.wait_ge(ln_rs[r].sem, ln_rs[r].at(b, 1))
                for m in range(MT):
                    last = v_.tensor_scalar(dst[:, m, :], src[:, m, :], mv[r][:, m, 0:1], rstd[r][:, m:m + 1],
                                            ALU.subtract, ALU.mult)
                return last

            x_absmax(0)
            for m in range(2):
                for c in range(4):
                    last = abs_part(m, c)
                step(last)
                abs_total(m)
                if m == 0:
                    matrix_part(0, 0)
                threshold(m)
                for c in range(4):
                    quantize(m, c)
                    if m == 0 and c == 1:
                        matrix_part(0, 1)
                if m == 0:
                    x_scales(0)
                    matrix_max(0)
                    matrix_scale(0, c_esc, ESC)
                    x_lo(0)
                    for h in range(H):
                        matrix_lo(A, 0, h)
            matrix_max(1)
            dve.wait_ge(small_ld.sem, small_ld.at(0, 2))

            def beside_first(j):
                if j == 0:
                    matrix_scale(1, c_asc, ASC)
                    x_scales_back()
                if j - 1 in B_SPLIT:
                    matrix_lo(Bm, 1, B_SPLIT.index(j - 1))
                if j in (7, 8, 9, 10):
                    last = abs_part(2, j - 7)
                    if j == 10:
                        step(last)
                        abs_total(2)
                if j == 13:
                    threshold(2)
                    step(v_.tensor_scalar(half_u, mean_w[:, 0:1], 0.5 / X2S, None, ALU.mult))
                    step(v_.tensor_tensor(gd, mean_w[:, 1:2], mean_w[:, 2:3], ALU.mult))
                    step(v_.tensor_scalar(gd, gd, mean_w[:, 0:1], DSC, ALU.mult, ALU.mult))

            def stages(i, att, cross, ffn, nxt, last_out):
                b, f = i - 1, i - 2

                def weight_scale(h):
                    dve.wait_ge(e_done.sem, e_done.at(i, h + 1))
                    v_.reciprocal(rs[:, h, :], sm[:, h, :]).then_inc(sum_inv.sem, 1)
                    dve.wait_ge(sum_inv.sem, sum_inv.at(i, h + 1))
                    v_.tensor_scalar(r4[:, h, :], rs[:, h, :], WTOP, None, ALU.mult).then_inc(wsc_rdy.sem, 1)

                def weight_lo(h):
                    dve.wait_ge(w_hi.sem, w_hi.at(i, h + 1))
                    for m in range(MT):
                        last = v_.scalar_tensor_tensor(ws[:, 1, h, m, :], we[:, h % 2, m, :], r4[:, h, m:m + 1],
                                                       ws[:, 0, h, m, :], ALU.mult, ALU.subtract)
                    last.then_inc(w_lo.sem, 1)

                def cross_max(t):
                    dve.wait_ge(s1_mm.sem, s1_mm.at(b, t + 1))
                    v_.tensor_reduce(xmx[:, t:t + 1], s1_bank(t, ffn)[:, :], AXX, ALU.max).then_inc(s1_max.sem, 1)

                def neg_max(grp):
                    dve.wait_ge(nt_mm.sem, nt_mm.at(b, grp + 1))
                    dve.wait_ge(nm_st.sem, nm_st.at(b - 1, 2 * MT))
                    v_.tensor_scalar(nm[:, grp, 0, :], bank["T"][0:GT, 0:P], -1.0 / MROW, None,
                                     ALU.mult).then_inc(nm_hi.sem, 1)
                    dve.wait_ge(nm_hi.sem, nm_hi.at(b, grp + 1))
                    v_.scalar_tensor_tensor(nm[:, grp, 1, :], bank["T"][0:GT, 0:P], -1.0 / MROW,
                                            nm[:, grp, 0, :], ALU.mult, ALU.subtract).then_inc(nm_lo.sem, 1)

                def cross_inv(batch, grp, half):
                    cols = slice(half * E // 2, (half + 1) * E // 2)
                    dve.wait_ge(den_mm.sem, den_mm.at(batch, grp + 1))
                    v_.reciprocal(den[:, cols], bank["T"][:, cols]).then_inc(den_inv.sem, 1)

                def cross_out(batch, grp):
                    dve.wait_ge(den_inv.sem, den_inv.at(batch, 2 * (grp + 1)))
                    dve.wait_ge(pv_mm.sem, pv_mm.at(batch, KT * (grp + 1)))
                    v_.tensor_tensor(den, bank["O"][:, :], den, ALU.mult).then_inc(o_read.sem, 1)
                    dve.wait_ge(o_read.sem, o_read.at(batch, grp + 1))
                    if grp == 0:
                        dve.wait_ge(x1_copy.sem, x1_copy.at(batch, 1))
                    v_.scalar_tensor_tensor(x1[:, grp, :], den, gam[:, 0:1], x1[:, grp, :], ALU.mult,
                                            ALU.add).then_inc(y2_rdy.sem, 1)

                for j, (kind, h, m) in enumerate(BLOCKS):
                    if cross:
                        for t in s1_tiles(i, j)[:1]:
                            cross_max(t)
                    if att:
                        bk = BANK[j]
                        if kind == "S":
                            dve.wait_ge(l_mm.sem, l_mm.at(i, j + 1))
                            v_.tensor_reduce(cm[:, h, :], bk[:, :].rearrange("p (m n) -> p m n", m=MT), AXX,
                                             ALU.max).then_inc(cmax.sem, 1)
                            dve.wait_ge(cmax.sem, cmax.at(i, h + 1))
                            v_.tensor_scalar(nb[:, h, :], cm[:, h, :], esc, -1.0, ALU.mult,
                                             ALU.mult).then_inc(bias_rdy.sem, 1)
                        else:
                            dve.wait_ge(gv_hi.sem, gv_hi.at(i, GV.index(j) + 1))
                            hi, lo = ([Gs[:, h % 2, s, 2 * m:2 * m + 2, :].rearrange("p k n -> p (k n)")
                                       for s in range(2)] if kind == "G" else [Vs[:, s, h, m, :] for s in range(2)])
                            v_.scalar_tensor_tensor(lo, bk[:, :], DOWN, hi, ALU.mult,
                                                    ALU.subtract).then_inc(gv_lo.sem, 1)
                        if j - 1 in SB:
                            weight_scale(SB.index(j - 1))
                        if j - 2 in SB:
                            weight_lo(SB.index(j - 2))
                    if cross:
                        for t in s1_tiles(i, j)[1:]:
                            cross_max(t)
                    if isinstance(i, int) and i == 0:
                        beside_first(j)
                    if isinstance(i, int) and i == 1 and j in QUANTIZE:
                        quantize(2, QUANTIZE.index(j))
                    if ffn and j in (1, 2):
                        cross_inv(f, 1, j - 1)
                    if ffn and j == 3:
                        cross_out(f, 1)
                    if last_out and j in (0, 5):
                        ln_stats(2, i - 3, x2, j // 5)
                    if last_out and j == 7:
                        ln_apply(2, i - 3, x2, x2).then_inc(out_rdy.sem, 1)
                    if ffn and j in (6, 7):
                        dve.wait_ge(y2_rdy.sem, y2_rdy.at(f, MT))
                        ln_stats(1, f, x1, j - 6)
                    if cross and j == 6:
                        dve.wait_ge(s2_exp.sem, s2_exp.at(b - 1, TILES))
                        v_.tensor_scalar(xsc, amr_c, XSC, None, ALU.mult).then_inc(xsc_rdy.sem, 1)
                    if att and j == 8:
                        dve.wait_ge(c_ld.sem, c_ld.at(i, 1))
                        v_.tensor_reduce(am_c, stage[:, :], AXX, ALU.max, apply_absolute_value=True).then_inc(
                            am_c_rdy.sem, 1)
                    if ffn and j == 10:
                        dve.wait_ge(out_st.sem, out_st.at(f - 1, 1))
                        ln_apply(1, f, x2, x1).then_inc(x2_rdy.sem, 1)
                    if att and j == 10:
                        dve.wait_ge(amr_c_rdy.sem, amr_c_rdy.at(i, 1))
                        v_.tensor_scalar(amr_c, amr_c, 1e-30, None, ALU.max).then_inc(cs_step.sem, 1)
                        dve.wait_ge(cs_step.sem, cs_step.at(i, 1))
                        v_.reciprocal(inv_c, amr_c).then_inc(cs_step.sem, 1)
                        dve.wait_ge(cs_step.sem, cs_step.at(i, 2))
                        v_.tensor_scalar(s_c, inv_c, KTOP, None, ALU.mult).then_inc(cs_step.sem, 1)
                    if ffn and j == 11:
                        dve.wait_ge(x2_hi.sem, x2_hi.at(f, 1))
                        v_.scalar_tensor_tensor(hl[:, 1], x2[:, :, :], X2S, hl[:, 0], ALU.mult,
                                                ALU.subtract).then_inc(x2_lo.sem, 1)
                    if cross and j == S1_TURN + 1:
                        neg_max(0)
                    if att and j == 13:
                        dve.wait_ge(k_hi.sem, k_hi.at(i, 1))
                        v_.scalar_tensor_tensor(ksplit[:, 1].rearrange("p m e -> p (m e)"), stage[:, :], s_c,
                                                ksplit[:, 0].rearrange("p m e -> p (m e)"), ALU.mult,
                                                ALU.subtract).then_inc(k_lo.sem, 1)
                if nxt and not cross:
                    x_absmax(i + 1)
                    x_scales(i + 1)
                    x_lo(i + 1)
                if att:
                    dve.wait_ge(xb_rdy.sem, xb_rdy.at(i, 1))
                    for n in range(MT):
                        dve.wait_ge(l_mm.sem, l_mm.at(i, NBLK + n + 1))
                        v_.scalar_tensor_tensor(xn[:, n, :], BANK[NBLK + n][:, :], asc, xn[:, n, :], ALU.mult,
                                                ALU.add).then_inc(y1_rdy.sem, 1)

                if nxt and not cross:
                    dve.wait_ge(y1_rdy.sem, y1_rdy.at(i, MT))
                    x_scales_back()

                def pair_t(u):
                    dve.wait_ge(th_rdy.sem, th_rdy.at(f, u + 1))
                    v_.scalar_tensor_tensor(th[:, u % 2, :], th[:, u % 2, :], 1.0, bank["U"][:, :], ALU.add,
                                            ALU.mult).then_inc(t_rdy.sem, 1)

                def pair_lo(u):
                    dve.wait_ge(h_hi.sem, h_hi.at(f, u + 1))
                    v_.tensor_tensor(hs[:, u % 2, 1].rearrange("p e n -> p (e n)"), th[:, u % 2, :],
                                     hs[:, u % 2, 0].rearrange("p e n -> p (e n)"),
                                     ALU.subtract).then_inc(h_lo.sem, 1)

                def pair_p(u):
                    dve.wait_ge(g_mm.sem, g_mm.at(f, u + 1))
                    dve.wait_ge(t_rdy.sem, t_rdy.at(f, u + 1))
                    v_.scalar_tensor_tensor(th[:, u % 2, :], th[:, u % 2, :], HS / 2, bank["G"][:, :], ALU.mult,
                                            ALU.mult).then_inc(p_rdy.sem, 1)

                def slot_maxes(u, *tiles):
                    if cross and u < S1_SLOTS:
                        for v in tiles:
                            cross_max(S1_BLOCKS + HG * u + v)

                def add_tiles(u):
                    for v in range(HG):
                        n = u * HG + v
                        dve.wait_ge(s2_exp.sem, s2_exp.at(b, n + 1))
                        if u % KT == 0:
                            dve.wait_ge(den_mm.sem, den_mm.at(b, u // KT))
                            v_.tensor_tensor(Psum[:, v, :], exp_tiles(u, ffn)[:, v, :],
                                             ones[:, 0:1].to_broadcast([P, E]), ALU.mult).then_inc(p_add.sem, 1)
                        else:
                            dve.wait_ge(p_add.sem, p_add.at(b, max(n - HG + 1, HG * S1_SLOTS)))
                            v_.tensor_tensor(Psum[:, v, :], Psum[:, v, :], exp_tiles(u, ffn)[:, v, :],
                                             ALU.add).then_inc(p_add.sem, 1)

                for u in range(8):
                    if ffn:
                        slot_maxes(u, 0)
                        if u == KT and cross:
                            cross_inv(b, 0, 0)
                        if u:
                            pair_lo(u - 1)
                        slot_maxes(u, 1)
                        pair_t(u)
                        if u == KT and cross:
                            cross_inv(b, 0, 1)
                            cross_out(b, 0)
                        slot_maxes(u, 2, 3)
                        pair_p(u)
                    elif cross:
                        slot_maxes(u, 0, 1, 2, 3)
                        if u == KT:
                            cross_inv(b, 0, 0)
                            cross_inv(b, 0, 1)
                            cross_out(b, 0)
                        if u >= S1_SLOTS:
                            add_tiles(u)
                    if u < MT and att:
                        dve.wait_ge(y1_rdy.sem, y1_rdy.at(i, MT))
                        ln_stats(0, i, xn, u)
                    if u == 2 and att:
                        ln_apply(0, i, xn, xn).then_inc(x1_rdy.sem, 1)
                    if u == S1_SLOTS - 1 and cross:
                        neg_max(1)
                    if u == 3 and att:
                        dve.wait_ge(q_hi.sem, q_hi.at(i, 1))
                        v_.scalar_tensor_tensor(hl[:, 1], xn[:, :, :], QS, hl[:, 0], ALU.mult,
                                                ALU.subtract).then_inc(q_lo.sem, 1)
                    if u == 4 and nxt and cross:
                        x_absmax(i + 1)
                    if u == 5 and nxt and cross:
                        x_scales(i + 1)
                        x_scales_back()
                    if u == 6 and nxt and cross:
                        x_lo(i + 1)
                if ffn:
                    pair_lo(PAIRS - 1)
                    dve.wait_ge(dn_mm.sem, dn_mm.at(f, PAIRS))
                    for n in range(MT):
                        v_.scalar_tensor_tensor(x2[:, n, :], L[n][:, :], gd, x2[:, n, :], ALU.mult,
                                                ALU.add).then_inc(y3_rdy.sem, 1)
                    dve.wait_ge(y3_rdy.sem, y3_rdy.at(f, MT))

            run_stages(dve, stages)


def kernel(x, ctx_2048, L0_attn_Wq, L0_attn_Wk, L0_attn_Wv, L0_attn_fc_w, L0_attn_fc_b, L0_xattn_gamma,
           L0_ffn_W_up, L0_ffn_W_gate, L0_ffn_W_down):
    import numpy as np
    import concourse.bacc as bacc
    from concourse.bass_utils import run_bass_kernel_spmd

    c = np.ascontiguousarray
    arrays = {
        "x": c(x), "xT": c(np.transpose(x, (0, 2, 1))),
        "ctx_n": c(ctx_2048), "ctx_t": c(np.transpose(ctx_2048, (0, 2, 1))),
        "wq": c(L0_attn_Wq), "wk": c(L0_attn_Wk), "wv": c(L0_attn_Wv),
        "fcT": c(np.transpose(L0_attn_fc_w)), "fcb": c(L0_attn_fc_b),
        "gamma": c(np.reshape(L0_xattn_gamma, (1,))),
        "wu": c(np.transpose(L0_ffn_W_up)), "wg": c(np.transpose(L0_ffn_W_gate)),
        "wd": c(np.transpose(L0_ffn_W_down)),
    }
    nc = bacc.Bacc("TRN2", target_bir_lowering=False, num_devices=1)
    args = [nc.dram_tensor("in_" + n, a.shape, mybir.dt.from_np(a.dtype), kind="ExternalInput").ap()
            for n, a in arrays.items()]
    result = nc.dram_tensor("result", x.shape, F32, kind="ExternalOutput").ap()
    decoder_layer(nc, *args, result)
    r = run_bass_kernel_spmd(nc, [{"in_" + n: a for n, a in arrays.items()}], core_ids=[0])
    return r.results[0]["result"]
```
